# Optimizing a Trainium2 kernel written in Bass

```python
import numpy as np
import jax
import jax.numpy as jnp

def _softmax(x, axis=-1):
    return jax.nn.softmax(x, axis=axis)

def _gelu(x):
    return jax.nn.gelu(x, approximate=True)

def _silu(x):
    return jax.nn.silu(x)

def _sigmoid(x):
    return jax.nn.sigmoid(x)

def _layernorm(x, axis=-1, eps=1e-05):
    m = jnp.mean(x, axis=axis, keepdims=True)
    v = jnp.var(x, axis=axis, keepdims=True)
    return (x - m) / jnp.sqrt(v + eps)

def _scatter_add(tgt, idx, src, axis=0):
    return tgt.at[idx].add(src)

def _segment_sum(src, seg, n):
    return jax.ops.segment_sum(src, seg, n)
kernel_name = 'mk_dlrm_tower_d1_rec_r8_06b210'

def setup_inputs(seed: int=0):
    np.random.seed(seed)
    _w = jnp.asarray

    def _rec_inputs():
        import jax
        import jax.numpy as jnp
        _tk = jax.random.key(seed)
        dense_ctx = jax.random.normal(jax.random.fold_in(_tk, 190), (2048, 16), jnp.float32)
        ids = jnp.stack([jax.random.randint(jax.random.fold_in(_tk, 200 + f), (2048,), 0, v, jnp.int32) for f, v in enumerate([12500, 1250, 1000, 12500, 12500, 1000, 12500, 125000, 12500, 1250, 1000, 1000, 12500, 1250, 12500, 1000, 1250, 1250, 1000, 12500, 1000, 1000, 1250, 1250, 1250, 1250, 1000])], axis=1)
        tbl_0 = 0.05 * jax.random.normal(jax.random.fold_in(_tk, 500 + 0), (12500, 128), jnp.float32)
        tbl_1 = 0.05 * jax.random.normal(jax.random.fold_in(_tk, 500 + 1), (1250, 128), jnp.float32)
        tbl_2 = 0.05 * jax.random.normal(jax.random.fold_in(_tk, 500 + 2), (1000, 128), jnp.float32)
        tbl_3 = 0.05 * jax.random.normal(jax.random.fold_in(_tk, 500 + 3), (12500, 128), jnp.float32)
        tbl_4 = 0.05 * jax.random.normal(jax.random.fold_in(_tk, 500 + 4), (12500, 128), jnp.float32)
        tbl_5 = 0.05 * jax.random.normal(jax.random.fold_in(_tk, 500 + 5), (1000, 128), jnp.float32)
        tbl_6 = 0.05 * jax.random.normal(jax.random.fold_in(_tk, 500 + 6), (12500, 128), jnp.float32)
        tbl_7 = 0.05 * jax.random.normal(jax.random.fold_in(_tk, 500 + 7), (125000, 128), jnp.float32)
        tbl_8 = 0.05 * jax.random.normal(jax.random.fold_in(_tk, 500 + 8), (12500, 128), jnp.float32)
        tbl_9 = 0.05 * jax.random.normal(jax.random.fold_in(_tk, 500 + 9), (1250, 128), jnp.float32)
        tbl_10 = 0.05 * jax.random.normal(jax.random.fold_in(_tk, 500 + 10), (1000, 128), jnp.float32)
        tbl_11 = 0.05 * jax.random.normal(jax.random.fold_in(_tk, 500 + 11), (1000, 128), jnp.float32)
        tbl_12 = 0.05 * jax.random.normal(jax.random.fold_in(_tk, 500 + 12), (12500, 128), jnp.float32)
        tbl_13 = 0.05 * jax.random.normal(jax.random.fold_in(_tk, 500 + 13), (1250, 128), jnp.float32)
        tbl_14 = 0.05 * jax.random.normal(jax.random.fold_in(_tk, 500 + 14), (12500, 128), jnp.float32)
        tbl_15 = 0.05 * jax.random.normal(jax.random.fold_in(_tk, 500 + 15), (1000, 128), jnp.float32)
        tbl_16 = 0.05 * jax.random.normal(jax.random.fold_in(_tk, 500 + 16), (1250, 128), jnp.float32)
        tbl_17 = 0.05 * jax.random.normal(jax.random.fold_in(_tk, 500 + 17), (1250, 128), jnp.float32)
        tbl_18 = 0.05 * jax.random.normal(jax.random.fold_in(_tk, 500 + 18), (1000, 128), jnp.float32)
        tbl_19 = 0.05 * jax.random.normal(jax.random.fold_in(_tk, 500 + 19), (12500, 128), jnp.float32)
        tbl_20 = 0.05 * jax.random.normal(jax.random.fold_in(_tk, 500 + 20), (1000, 128), jnp.float32)
        tbl_21 = 0.05 * jax.random.normal(jax.random.fold_in(_tk, 500 + 21), (1000, 128), jnp.float32)
        tbl_22 = 0.05 * jax.random.normal(jax.random.fold_in(_tk, 500 + 22), (1250, 128), jnp.float32)
        tbl_23 = 0.05 * jax.random.normal(jax.random.fold_in(_tk, 500 + 23), (1250, 128), jnp.float32)
        tbl_24 = 0.05 * jax.random.normal(jax.random.fold_in(_tk, 500 + 24), (1250, 128), jnp.float32)
        tbl_25 = 0.05 * jax.random.normal(jax.random.fold_in(_tk, 500 + 25), (1250, 128), jnp.float32)
        tbl_26 = 0.05 * jax.random.normal(jax.random.fold_in(_tk, 500 + 26), (1000, 128), jnp.float32)
        _rk = jax.random.fold_in(_tk, 7)
        W_top1 = 0.0521996 * jax.random.normal(jax.random.fold_in(_tk, 801), (367, 512), jnp.float32)
        W_top2 = 0.0441942 * jax.random.normal(jax.random.fold_in(_tk, 802), (512, 256), jnp.float32)
        W_top3 = 0.0625 * jax.random.normal(jax.random.fold_in(_tk, 803), (256, 1), jnp.float32)
        b_top1 = jnp.zeros((512,), jnp.float32)
        b_top2 = jnp.zeros((256,), jnp.float32)
        return (dense_ctx, ids, tbl_0, tbl_1, tbl_2, tbl_3, tbl_4, tbl_5, tbl_6, tbl_7, tbl_8, tbl_9, tbl_10, tbl_11, tbl_12, tbl_13, tbl_14, tbl_15, tbl_16, tbl_17, tbl_18, tbl_19, tbl_20, tbl_21, tbl_22, tbl_23, tbl_24, tbl_25, tbl_26, W_top1, b_top1, W_top2, b_top2, W_top3)
    dense_ctx, ids, tbl_0, tbl_1, tbl_2, tbl_3, tbl_4, tbl_5, tbl_6, tbl_7, tbl_8, tbl_9, tbl_10, tbl_11, tbl_12, tbl_13, tbl_14, tbl_15, tbl_16, tbl_17, tbl_18, tbl_19, tbl_20, tbl_21, tbl_22, tbl_23, tbl_24, tbl_25, tbl_26, W_top1, b_top1, W_top2, b_top2, W_top3 = _rec_inputs()

    def _L0_rec_setup():
        import jax, jax.numpy as jnp
        import numpy as np

        def _tri_indices(num_feas):
            return np.array([i * num_feas + j for j in range(1, num_feas) for i in range(j)], dtype=np.int32)
        key = jax.random.key(seed)
        batch, num_feas, embed_dim = (2048, 27, 128)
        inputs = jax.random.normal(key, (batch, num_feas, embed_dim), dtype=jnp.float32)
        return {'inputs': inputs, 'num_feas': num_feas}
    _L0_rec_all = _L0_rec_setup()
    _L0_rec_in = {k: v for k, v in _L0_rec_all.items() if k in ()}
    del _L0_rec_all
    return {'dense_ctx': dense_ctx, 'ids': ids, 'tbl_0': tbl_0, 'tbl_1': tbl_1, 'tbl_2': tbl_2, 'tbl_3': tbl_3, 'tbl_4': tbl_4, 'tbl_5': tbl_5, 'tbl_6': tbl_6, 'tbl_7': tbl_7, 'tbl_8': tbl_8, 'tbl_9': tbl_9, 'tbl_10': tbl_10, 'tbl_11': tbl_11, 'tbl_12': tbl_12, 'tbl_13': tbl_13, 'tbl_14': tbl_14, 'tbl_15': tbl_15, 'tbl_16': tbl_16, 'tbl_17': tbl_17, 'tbl_18': tbl_18, 'tbl_19': tbl_19, 'tbl_20': tbl_20, 'tbl_21': tbl_21, 'tbl_22': tbl_22, 'tbl_23': tbl_23, 'tbl_24': tbl_24, 'tbl_25': tbl_25, 'tbl_26': tbl_26, 'W_top1': W_top1, 'b_top1': b_top1, 'W_top2': W_top2, 'b_top2': b_top2, 'W_top3': W_top3}

def reference(dense_ctx, ids, tbl_0, tbl_1, tbl_2, tbl_3, tbl_4, tbl_5, tbl_6, tbl_7, tbl_8, tbl_9, tbl_10, tbl_11, tbl_12, tbl_13, tbl_14, tbl_15, tbl_16, tbl_17, tbl_18, tbl_19, tbl_20, tbl_21, tbl_22, tbl_23, tbl_24, tbl_25, tbl_26, W_top1, b_top1, W_top2, b_top2, W_top3):
    import jax
    import jax.numpy as jnp

    def _L0_rec_ref(inputs, num_feas):
        import jax, jax.numpy as jnp
        import numpy as np

        def _tri_indices(num_feas):
            return np.array([i * num_feas + j for j in range(1, num_feas) for i in range(j)], dtype=np.int32)
        dot = jnp.einsum('bnd,bmd->bnm', inputs, inputs)
        idx = jnp.asarray(_tri_indices(num_feas))
        flat = dot.reshape(inputs.shape[0], num_feas * num_feas)
        return flat[:, idx]
    e = jnp.stack([tbl_0[ids[:, 0]], tbl_1[ids[:, 1]], tbl_2[ids[:, 2]], tbl_3[ids[:, 3]], tbl_4[ids[:, 4]], tbl_5[ids[:, 5]], tbl_6[ids[:, 6]], tbl_7[ids[:, 7]], tbl_8[ids[:, 8]], tbl_9[ids[:, 9]], tbl_10[ids[:, 10]], tbl_11[ids[:, 11]], tbl_12[ids[:, 12]], tbl_13[ids[:, 13]], tbl_14[ids[:, 14]], tbl_15[ids[:, 15]], tbl_16[ids[:, 16]], tbl_17[ids[:, 17]], tbl_18[ids[:, 18]], tbl_19[ids[:, 19]], tbl_20[ids[:, 20]], tbl_21[ids[:, 21]], tbl_22[ids[:, 22]], tbl_23[ids[:, 23]], tbl_24[ids[:, 24]], tbl_25[ids[:, 25]], tbl_26[ids[:, 26]]], axis=1)
    z = _L0_rec_ref(e, 27)
    z = z.reshape(z.shape[0], -1)
    h = jnp.concatenate([z, dense_ctx], axis=1)
    h = jnp.maximum(h @ W_top1 + b_top1, 0.0)
    h = jnp.maximum(h @ W_top2 + b_top2, 0.0)
    y = h @ W_top3
    return y

_drawn_inputs = setup_inputs


def setup_inputs(seed=0):
    import zlib

    import numpy as np

    out = dict(_drawn_inputs(seed))
    spreads = {'b_top1': (0.0, 0.1), 'b_top2': (0.0, 0.1)}
    factors = {}
    for name, (base, spread) in spreads.items():
        noise = np.random.default_rng([zlib.crc32(name.encode()), seed]).standard_normal(out[name].shape)
        drawn = base * np.exp(spread * noise) if base else spread * noise
        out[name] = jnp.asarray(drawn.astype(out[name].dtype))
    for name, factor in factors.items():
        out[name] = (out[name] * factor).astype(out[name].dtype)
    return out
```

```python
import concourse.bass as bass
from concourse import mybir
from contextlib import ExitStack


def dlrm_tower(nc, dense_ctx, ids, tables, w_top1, b_top1, w_top2, b_top2, w_top3, out):
    fp32 = mybir.dt.float32
    f32r = mybir.dt.float32r
    fp16 = mybir.dt.float16
    i32 = mybir.dt.int32
    ALU = mybir.AluOpType
    ACT = mybir.ActivationFunctionType

    P = 128
    BATCH, NF = ids.shape
    D = tables[0].shape[1]
    ND = dense_ctx.shape[1]
    H1 = w_top1.shape[1]
    H2 = w_top2.shape[1]
    T = 4
    MACRO = T * P
    NM = BATCH // MACRO
    NJ = NF - 1
    NPAIR = NF * NJ // 2
    KZ = NPAIR + ND + 1
    ZC = [(c, min(P, KZ - c)) for c in range(0, KZ, P)]
    ROW = 32
    S = P // ROW
    GT = P // S
    GH = GT // 2

    ONEHOT = [5, 10, 15, 20, 11, 21, 18, 26]
    NO = len(ONEHOT)
    VR = tables[ONEHOT[0]].shape[0]
    KT = 8
    RP = VR // KT
    HMASK = -(1 << 12)
    RING = 4
    UNIT = 4

    BATCHES = [[0, 1, 2, 3], [6, 7, 8], [12, 13, 16, 17], [22, 23, 24, 25], [4, 9, 14, 19]]
    SLOT = {f: n for n, f in enumerate(f for b in BATCHES for f in b)}
    NG = len(SLOT)
    NB = len(BATCHES)

    ZB = [list(range(j, min(j + 4, NJ))) for j in range(0, NJ, 4)]
    NZ = len(ZB) + len(ZC)
    H1C = H1 // P
    H2C = H2 // P
    CHUNKS = ([[("turn", n) for n in range(b, min(b + 2, len(ZB)))] for b in range(0, len(ZB), 2)]
              + [[("pairs", 0), ("pairs", 1)], [("pairs", 2)]]
              + [[("hidden1", n)] for n in range(H1C)] + [[("hidden2", n)] for n in range(H2C)] + [[("score", 0)]])
    NH = H1C + H2C + 1

    OH = [("ids", 0), ("ids", 1)]
    for n in range(NO):
        OH += [("rows", n, k) for k in range(0, KT, UNIT)]
        if n + 2 < NO:
            OH.append(("ids", n + 2))
    OH_GROUPS = [OH[0:3]]
    for step in OH[3:]:
        if step[0] == "rows":
            OH_GROUPS.append([step])
        else:
            OH_GROUPS[-1].append(step)

    MIXED = []
    for n in range(max(len(CHUNKS), len(OH_GROUPS))):
        MIXED += CHUNKS[n] if n < len(CHUNKS) else []
        MIXED += OH_GROUPS[n] if n < len(OH_GROUPS) else []
    ALONE = [step for chunk in CHUNKS for step in chunk]

    A_TILES = T * NB
    A_OH = {}
    for step in OH:
        if step[0] == "ids":
            A_OH[step] = len(A_OH)
        elif step[2] == KT - UNIT:
            A_OH[("rows", step[1])] = len(A_OH)
    NA_OH = len(A_OH)
    NA = A_TILES + NA_OH
    NF_OH = NO
    NFULL = A_TILES + NF_OH

    ctx = ExitStack()
    with ctx:
        def sb(name, shape, dt):
            return ctx.enter_context(nc.sbuf_tensor(name, shape, dt))

        def sem(name):
            return ctx.enter_context(nc.semaphore(name))

        ids_sb = sb("ids_sb", [P, NM, T, NF], i32)
        ids_now = sb("ids_now", [P, T, NF], i32)
        free = sb("free", [P, 4], fp32)
        ids16 = sb("ids16", [P, T, NO], fp16)
        idsb = sb("idsb", [P, 2, MACRO], fp16)
        rowid = sb("rowid", [P, KT], fp32)
        ident = sb("ident", [P, P], fp32)
        ident16 = sb("ident16", [P, P], fp16)
        emb = sb("emb", [P, T, NG, D], fp32)
        EW = P * NF + ROW - NF
        emb_t = sb("emb_t", [D, T, EW], fp32)
        tab_hi = sb("tab_hi", [P, NO, KT, D], f32r)
        tab_lo = sb("tab_lo", [P, NO, KT, D], f32r)
        onehot = sb("onehot", [P, RING, MACRO], f32r)
        dots = sb("dots", [P, NJ * T * GT], fp32)
        dots_v = dots[:, :].rearrange("p (j g) -> p j g", j=NJ)
        z = sb("z", [P, S, KZ], fp32)
        z_t = sb("z_t", [P, len(ZC), MACRO], fp32)
        zd = sb("zd", [P, NM, S, ND], fp32)
        w1 = sb("w1", [P, len(ZC), H1], fp32)
        w2 = sb("w2", [P, H1C, H2], fp32)
        w3 = sb("w3", [P, H2C], fp32)
        b2 = sb("b2", [P, H2C], fp32)
        y = sb("y", [1, MACRO], fp32)
        h1 = dots[:, 0:H1C * MACRO].rearrange("p (c n) -> p c n", c=H1C)
        h2 = z_t[:, 0:H2C, :]
        NRAW = 3
        raw = [dots[0:RP, n * KT * D:(n + 1) * KT * D] for n in range(NRAW)]
        high = [z[0:RP, :, :].rearrange("p s k -> p (s k)")[:, 0:KT * D],
                z_t[0:RP, :, :].rearrange("p s k -> p (s k)")[:, 0:KT * D]]

        turned = [ctx.enter_context(nc.psum_tensor(f"turned{n}", [P, 512], fp32)) for n in range(2)]
        dot_ps = [ctx.enter_context(nc.psum_tensor(f"dot_ps{n}", [P, 512], fp32)) for n in range(2)]
        z_ps = [ctx.enter_context(nc.psum_tensor(f"z_ps{n}", [P, 512], fp32)) for n in range(2)]
        h_ps = [ctx.enter_context(nc.psum_tensor(f"h_ps{n}", [P, 512], fp32)) for n in range(2)]

        ids_in = sem("ids_in")
        weights_in = sem("weights_in")
        dense_in = sem("dense_in")
        raw_in = [sem(f"raw_in{n}") for n in range(NRAW)]
        masked = sem("masked")
        hi_done = sem("hi_done")
        lo_done = sem("lo_done")
        ident_zero = sem("ident_zero")
        ident_done = sem("ident_done")
        ident16_done = sem("ident16_done")
        rowid_done = sem("rowid_done")
        pads_done = sem("pads_done")
        ids16_done = sem("ids16_done")
        gathered = [[sem(f"gathered{t}_{b}") for b in range(NB)] for t in range(T)]
        tile_open = [sem(f"tile_open{t}") for t in range(T)]
        turned_full = sem("turned_full")
        turned_out = sem("turned_out")
        onehot_full = sem("onehot_full")
        onehot_used = sem("onehot_used")
        dot_full = sem("dot_full")
        dot_out = sem("dot_out")
        z_full = sem("z_full")
        z_out = sem("z_out")
        h_full = sem("h_full")
        h_out = sem("h_out")
        y_sent = sem("y_sent")

        FREE = 1

        block = ctx.enter_context(nc.Block())

        def batch_view(ap, feats):
            step = feats[1] - feats[0]
            if feats[-1] - feats[0] == step * (len(feats) - 1):
                return ap[:, feats[0]:feats[-1] + 1:step, :]
            jump = feats[2] - feats[0]
            return ap[:, feats[0]:feats[0] + 2 * jump, :].rearrange("d (a b) p -> d a b p", a=2)[:, :, 0:2, :]

        @block.sync
        def _(sp):
            sp.dma_start(ids_sb[:, :, :, :],
                         ids.rearrange("(m p t) f -> p m (t f)", m=NM, t=T).rearrange("p m (t f) -> p m t f", t=T)
                         ).then_inc(ids_in, 16)
            for n, f in enumerate(ONEHOT):
                if n >= NRAW:
                    sp.wait_ge(lo_done, n - NRAW + 1)
                sp.dma_start(raw[n % NRAW], tables[f].rearrange("(p k) d -> p (k d)", k=KT)).then_inc(raw_in[n % NRAW], 16)
            with sp.Fori(0, NM) as m:
                sp.wait_ge(h_out, FREE + NH * (m + 1))
                sp.dma_start(out[bass.ds(m * MACRO, MACRO), :].rearrange("n o -> o n"), y[:, :]).then_inc(y_sent, 16)
            sp.wait_ge(y_sent, 16 * (NM + 1))

        @block.gpsimd
        def _(pool):
            nc.gpsimd.iota(rowid[0:RP, :], [[1, KT]], base=0, channel_multiplier=KT,
                           allow_small_or_imprecise_dtypes=True).then_inc(rowid_done, 1)
            pool.wait_ge(ident_zero, 1)
            nc.gpsimd.affine_select(out=ident[:, :], in_=ident[:, :], compare_op=ALU.not_equal, fill=1.0, base=0,
                                    pattern=[[-1, P]], channel_multiplier=1).then_inc(ident_done, 1)
            with pool.Fori(1, NM + 1) as opened:
                for t in range(T):
                    pool.wait_ge(ids_in, 16)
                    pool.wait_ge(tile_open[t], opened)
                    for b, feats in enumerate(BATCHES):
                        for f in feats:
                            nc.gpsimd.indirect_dma_start(
                                out=emb[:, t, SLOT[f], :], out_offset=None, in_=tables[f],
                                in_offset=bass.IndirectOffsetOnAxis(ap=ids_now[:, t, f:f + 1], axis=0),
                            ).then_inc(gathered[t][b], 16)

        @block.tensor
        def _(pe):
            def onehot_step(m, step):
                if step[0] == "ids":
                    _, n = step
                    use = A_OH[step]
                    if n == 0:
                        pe.wait_ge(ids16_done, m + 1)
                    if not (isinstance(m, int) and use < 2):
                        pe.wait_ge(turned_out, NA * m + use - 1)
                    bank = turned[use % 2]
                    for t in range(T):
                        last = nc.tensor.matmul(bank[:, t * P:(t + 1) * P],
                                                ids16[:, t, n:n + 1].to_broadcast([P, P]), ident16[:, :],
                                                start=True, stop=True)
                    last.then_inc(turned_full, 1)
                    return
                _, n, k0 = step
                use = A_OH[("rows", n)]
                bank = turned[use % 2]
                if k0 == 0:
                    if isinstance(m, int):
                        pe.wait_ge(hi_done, n + 1)
                        pe.wait_ge(lo_done, n + 1)
                    pe.wait_ge(turned_out, NA * m + use - 1)
                for k in range(k0, k0 + UNIT):
                    at = KT * n + k
                    pe.wait_ge(onehot_full, NO * KT * m + at + 1)
                    nc.tensor.matmul(bank[:, :], tab_hi[0:RP, n, k, :], onehot[0:RP, at % RING, :],
                                     start=(k == 0), stop=False)
                    last = nc.tensor.matmul(bank[:, :], tab_lo[0:RP, n, k, :], onehot[0:RP, at % RING, :],
                                            start=False, stop=(k == KT - 1))
                    last.then_inc(onehot_used, 1)

            def tile(m, t):
                for b, feats in enumerate(BATCHES):
                    use = NB * t + b
                    pe.wait_ge(gathered[t][b], 16 * len(feats) * (m + 1))
                    pe.wait_ge(turned_out, NA_OH + NA * m + use - 1)
                    for q, f in enumerate(feats):
                        last = nc.tensor.transpose(turned[use % 2][:, q * P:(q + 1) * P], emb[:, t, SLOT[f], :],
                                                   ident[:, :])
                    last.then_inc(turned_full, 1)
                last_turned = NB * (t + 1)
                pe.wait_ge(turned_out, NA_OH + NA * m + last_turned)
                for half in range(2):
                    use = 2 * t + half
                    pe.wait_ge(dot_out, FREE + 2 * T * m + max(use - 1, 0))
                    for g in range(GH):
                        for s in range(S):
                            at = ((half * GH + g) * S + s) * NF
                            last = nc.tensor.matmul(dot_ps[half][ROW * s:ROW * (s + 1), g * NJ:(g + 1) * NJ],
                                                    emb_t[:, t, at:at + ROW], emb_t[:, t, at + 1:at + NF],
                                                    start=True, stop=True, tile_position=(0, ROW * s))
                    last.then_inc(dot_full, 1)

            def mlp_step(m, step):
                kind, n = step
                if kind in ("turn", "pairs"):
                    use = n if kind == "turn" else len(ZB) + n
                    bank = z_ps[use % 2]
                    if step == ("turn", 0):
                        pe.wait_ge(dot_out, FREE + 2 * T * (m + 1))
                    if step == ("pairs", 0):
                        pe.wait_ge(z_out, FREE + NZ * m + len(ZB))
                    pe.wait_ge(z_out, FREE + NZ * m + max(use - 1, 0))
                    if kind == "turn":
                        for q, j in enumerate(ZB[n]):
                            last = nc.tensor.transpose(bank[:, q * P:(q + 1) * P], dots_v[:, j, :], ident[:, :])
                    else:
                        c, w = ZC[n]
                        for s in range(S):
                            last = nc.tensor.transpose(bank[0:w, s * P:(s + 1) * P], z[:, s, c:c + w], ident[:, :])
                    last.then_inc(z_full, 1)
                    return
                use = {"hidden1": 0, "hidden2": H1C, "score": H1C + H2C}[kind] + n
                bank = h_ps[use % 2]
                if step == ("hidden1", 0):
                    pe.wait_ge(z_out, FREE + NZ * (m + 1))
                before = {"hidden1": max(n - 1, 0), "hidden2": H1C, "score": H1C + H2C}[kind]
                pe.wait_ge(h_out, FREE + NH * m + before)
                if kind == "hidden1":
                    for c, (_, w) in enumerate(ZC):
                        last = nc.tensor.matmul(bank[:, :], w1[0:w, c, n * P:(n + 1) * P], z_t[0:w, c, :],
                                                start=(c == 0), stop=(c == len(ZC) - 1))
                elif kind == "hidden2":
                    for c in range(H1C):
                        last = nc.tensor.matmul(bank[:, :], w2[:, c, n * P:(n + 1) * P], h1[:, c, :],
                                                start=(c == 0), stop=(c == H1C - 1))
                else:
                    for c in range(H2C):
                        last = nc.tensor.matmul(bank[0:1, :], w3[:, c:c + 1], h2[:, c, :],
                                                start=(c == 0), stop=(c == H2C - 1))
                last.then_inc(h_full, 1)

            pe.wait_ge(ident16_done, 1)
            for step in OH:
                onehot_step(0, step)
            pe.wait_ge(ident_done, 1)
            pe.wait_ge(pads_done, 1)
            pe.wait_ge(weights_in, 16 * 7)
            with pe.Fori(0, NM - 1) as m:
                for t in range(T):
                    tile(m, t)
                for step in MIXED:
                    if step[0] in ("ids", "rows"):
                        onehot_step(m + 1, step)
                    else:
                        mlp_step(m, step)
            for t in range(T):
                tile(NM - 1, t)
            for step in ALONE:
                mlp_step(NM - 1, step)

        @block.scalar
        def _(act):
            for c, (c0, w) in enumerate(ZC):
                rows = min(w, NPAIR + ND - c0)
                act.dma_start(w1[0:rows, c, :], w_top1[c0:c0 + rows, :]).then_inc(weights_in, 16)
            act.dma_start(w1[ZC[-1][1] - 1:ZC[-1][1], len(ZC) - 1, :],
                          b_top1.rearrange("(o h) -> o h", o=1)).then_inc(weights_in, 16)
            act.dma_start(w2[:, :, :], w_top2.rearrange("(c p) h -> p c h", p=P)).then_inc(weights_in, 16)
            with nc.allow_non_contiguous_dma(reason="256 single words, once"):
                act.dma_start(w3[:, :], w_top3.rearrange("(c p) o -> p (c o)", p=P)).then_inc(weights_in, 16)
                act.dma_start(b2[:, :], b_top2.rearrange("(c p) -> p c", p=P)).then_inc(weights_in, 16)
            dense_v = dense_ctx.rearrange("(m g s t) c -> t m g s c", m=NM, g=GT, s=S, t=T)
            for t in range(T):
                for m in range(NM):
                    act.dma_start(zd[t * GT:(t + 1) * GT, m, :, :], dense_v[t, m]).then_inc(dense_in, 16)

            def ids_spread(m, n):
                act.wait_ge(turned_full, NFULL * m + n + 1)
                if not (isinstance(m, int) and n < 2):
                    act.wait_ge(onehot_full, KT * (NO * m + n - 1))
                nc.scalar.copy(idsb[:, n % 2, :], turned[A_OH[("ids", n)] % 2][:, :]).then_inc(turned_out, 1)

            def onehot_out(m, n):
                act.wait_ge(onehot_used, KT * (NO * m + n + 1))
                f = ONEHOT[n]
                nc.scalar.copy(emb_t[:, :, 0:P * NF].rearrange("d t (p f) -> d t p f", f=NF)[:, :, :, f],
                               turned[A_OH[("rows", n)] % 2][:, :].rearrange("d (t p) -> d t p", t=T)
                               ).then_inc(turned_out, 1)

            def onehot_step(m, step):
                if step[0] == "ids":
                    ids_spread(m, step[1])
                elif step[2] + UNIT == KT:
                    onehot_out(m, step[1])

            def tile(m, t):
                for b, feats in enumerate(BATCHES):
                    use = NB * t + b
                    act.wait_ge(turned_full, NF_OH + NFULL * m + use + 1)
                    dst = batch_view(emb_t[:, t, 0:P * NF].rearrange("d (p f) -> d f p", f=NF), feats)
                    src = turned[use % 2][:, 0:len(feats) * P]
                    if len(dst.shape) == 4:
                        src = src.rearrange("d (a b p) -> d a b p", a=2, b=2)
                    else:
                        src = src.rearrange("d (q p) -> d q p", p=P)
                    nc.scalar.copy(dst, src).then_inc(turned_out, 1)

            def mlp_step(m, step):
                kind, n = step
                if kind not in ("hidden1", "hidden2", "score"):
                    return
                use = {"hidden1": 0, "hidden2": H1C, "score": H1C + H2C}[kind] + n
                bank = h_ps[use % 2]
                act.wait_ge(h_full, NH * m + use + 1)
                if kind == "hidden1":
                    nc.scalar.activation(h1[:, n, :], bank[:, :], ACT.Relu).then_inc(h_out, 1)
                elif kind == "hidden2":
                    nc.scalar.activation(h2[:, n, :], bank[:, :], ACT.Relu, bias=b2[:, n:n + 1]).then_inc(h_out, 1)
                else:
                    act.wait_ge(y_sent, 16 * (m + 1))
                    nc.scalar.copy(y[:, :].rearrange("o (g s t) -> o s t g", s=S, t=T),
                                   bank[0:1, :].rearrange("o (s t g) -> o s t g", s=S, t=T)).then_inc(h_out, 1)

            def table_high(n):
                act.wait_ge(masked, n + 1)
                nc.scalar.copy(tab_hi[0:RP, n, :, :], high[n % 2].rearrange("p (k d) -> p k d", k=KT)
                               ).then_inc(hi_done, 1)

            for n in range(NO):
                table_high(n) if n < 2 else None
            for step in OH:
                if step[0] == "rows" and step[2] == 0 and step[1] + 2 < NO:
                    table_high(step[1] + 2)
                onehot_step(0, step)
            act.wait_ge(weights_in, 16 * 7)
            with act.Fori(0, NM - 1) as m:
                for t in range(T):
                    tile(m, t)
                for step in MIXED:
                    if step[0] in ("ids", "rows"):
                        onehot_step(m + 1, step)
                    else:
                        mlp_step(m, step)
            for t in range(T):
                tile(NM - 1, t)
            for step in ALONE:
                mlp_step(NM - 1, step)

        @block.vector
        def _(dve):
            def ids_to_fp16(m):
                nc.vector.tensor_copy(ids16[:, :, 0:4], ids_sb[:, bass.ds(m, 1), :, 5:21:5].rearrange("p m t f -> p (m t) f"))
                nc.vector.tensor_copy(ids16[:, :, 4:6], ids_sb[:, bass.ds(m, 1), :, 11:22:10].rearrange("p m t f -> p (m t) f"))
                nc.vector.tensor_copy(ids16[:, :, 6:8], ids_sb[:, bass.ds(m, 1), :, 18:27:8].rearrange("p m t f -> p (m t) f")
                                      ).then_inc(ids16_done, 1)

            def onehot_step(m, step):
                if step[0] == "ids":
                    return
                _, n, k0 = step
                if k0 == 0:
                    dve.wait_ge(turned_out, NA * m + A_OH[("ids", n)] + 1)
                for k in range(k0, k0 + UNIT):
                    at = KT * n + k
                    if not (isinstance(m, int) and at < RING):
                        dve.wait_ge(onehot_used, NO * KT * m + at - RING + 1)
                    nc.vector.tensor_scalar(onehot[0:RP, at % RING, :], idsb[0:RP, n % 2, :], rowid[0:RP, k:k + 1],
                                            None, ALU.is_equal).then_inc(onehot_full, 1)

            def open_tile(m, t):
                nc.vector.tensor_copy(ids_now[:, t, :], ids_sb[:, bass.ds(m, 1), t, :].rearrange("p m f -> p (m f)")
                                      ).then_inc(tile_open[t], 1)

            def tile(m, t):
                for half in range(2):
                    dve.wait_ge(dot_full, 2 * T * m + 2 * t + half + 1)
                    if half == 0 and not isinstance(m, int):
                        open_tile(m + 1, t)
                    g0 = t * GT + half * GH
                    nc.vector.tensor_copy(dots_v[:, :, g0:g0 + GH].rearrange("p j g -> p g j"),
                                          dot_ps[half][:, 0:GH * NJ].rearrange("p (g j) -> p g j", j=NJ)
                                          ).then_inc(dot_out, 1)

            def mlp_step(m, step):
                kind, n = step
                if kind == "turn":
                    dve.wait_ge(z_full, NZ * m + n + 1)
                    if n == 0:
                        nc.vector.tensor_copy(z[:, :, NPAIR:NPAIR + ND],
                                              zd[:, bass.ds(m, 1), :, :].rearrange("p m s c -> p (m s) c"))
                    for q, j in enumerate(ZB[n]):
                        off = j * (j + 1) // 2
                        last = nc.vector.tensor_copy(
                            z[:, :, off:off + j + 1],
                            z_ps[n % 2][:, q * P:(q + 1) * P].rearrange("g (s i) -> g s i", s=S)[:, :, 0:j + 1])
                    last.then_inc(z_out, 1)
                elif kind == "pairs":
                    use = len(ZB) + n
                    w = ZC[n][1]
                    dve.wait_ge(z_full, NZ * m + use + 1)
                    nc.vector.tensor_copy(z_t[0:w, n, :], z_ps[use % 2][0:w, :]).then_inc(z_out, 1)

            nc.vector.memset(ident[:, :], 0.0).then_inc(ident_zero, 1)
            nc.vector.memset(free[:, 0:1], 0.0).then_inc(dot_out, FREE)
            nc.vector.memset(free[:, 1:2], 0.0).then_inc(z_out, FREE)
            nc.vector.memset(free[:, 2:3], 0.0).then_inc(h_out, FREE)
            nc.vector.memset(free[:, 3:4], 0.0).then_inc(y_sent, 16)
            nc.vector.memset(emb_t[:, :, P * NF:EW], 0.0).then_inc(pads_done, 1)
            dve.wait_ge(ids_in, 16)
            for t in range(T):
                open_tile(0, t)
            ids_to_fp16(0)
            dve.wait_ge(ident_done, 1)
            nc.vector.tensor_copy(ident16[:, :], ident[:, :]).then_inc(ident16_done, 1)
            dve.wait_ge(rowid_done, 1)

            def table_mask(n):
                dve.wait_ge(raw_in[n % NRAW], 16 * (n // NRAW + 1))
                if n >= 2:
                    dve.wait_ge(hi_done, n - 1)
                    dve.wait_ge(lo_done, n - 1)
                nc.vector.tensor_scalar(high[n % 2].bitcast(i32), raw[n % NRAW].bitcast(i32), HMASK, None,
                                        ALU.bitwise_and).then_inc(masked, 1)

            def table_low(n):
                dve.wait_ge(masked, n + 1)
                nc.vector.tensor_tensor(tab_lo[0:RP, n, :, :].rearrange("p k d -> p (k d)"), raw[n % NRAW],
                                        high[n % 2], ALU.subtract).then_inc(lo_done, 1)

            table_mask(0)
            table_mask(1)
            for step in OH:
                if step[0] == "rows" and step[2] == 0:
                    table_low(step[1])
                elif step[0] == "rows" and step[2] == UNIT and step[1] + 2 < NO:
                    table_mask(step[1] + 2)
                onehot_step(0, step)
            dve.wait_ge(hi_done, NO)
            dve.wait_ge(lo_done, NO)
            nc.vector.memset(z[:, :, KZ - 1:KZ], 1.0)
            dve.wait_ge(dense_in, 16 * T * NM)
            with dve.Fori(0, NM - 1) as m:
                ids_to_fp16(m + 1)
                for t in range(T):
                    tile(m, t)
                for step in MIXED:
                    if step[0] in ("ids", "rows"):
                        onehot_step(m + 1, step)
                    else:
                        mlp_step(m, step)
            for t in range(T):
                tile(NM - 1, t)
            for step in ALONE:
                mlp_step(NM - 1, step)


_INS = ["dense_ctx", "ids"] + [f"tbl_{i}" for i in range(27)] + ["W_top1", "b_top1", "W_top2", "b_top2", "W_top3"]


def kernel(**inputs):
    import numpy as _np
    import concourse.bacc as _bacc
    from concourse import mybir as _mybir
    from concourse.bass_utils import run_bass_kernel_spmd as _run

    nc = _bacc.Bacc("TRN2", target_bir_lowering=False, num_devices=1)
    arrays, args = {}, {}
    for name in _INS:
        a = _np.ascontiguousarray(inputs[name])
        arrays[f"in_{name}_dram"] = a
        args[name] = nc.dram_tensor(f"in_{name}_dram", a.shape, _mybir.dt.from_np(a.dtype), kind="ExternalInput").ap()
    batch = inputs["ids"].shape[0]
    out = nc.dram_tensor("out_0_dram", (batch, 1), _mybir.dt.float32, kind="ExternalOutput").ap()
    dlrm_tower(nc, args["dense_ctx"], args["ids"], [args[f"tbl_{i}"] for i in range(27)],
               args["W_top1"], args["b_top1"], args["W_top2"], args["b_top2"], args["W_top3"], out)
    r = _run(nc, [arrays], core_ids=[0])
    return r.results[0]["out_0_dram"]
```

```python
import concourse.bass as bass
from concourse import mybir
from contextlib import ExitStack


def dlrm_tower(nc, dense_ctx, ids, tables, w_top1, b_top1, w_top2, b_top2, w_top3, out):
    fp32 = mybir.dt.float32
    f32r = mybir.dt.float32r
    fp16 = mybir.dt.float16
    i32 = mybir.dt.int32
    ALU = mybir.AluOpType
    ACT = mybir.ActivationFunctionType

    P = 128
    BATCH, NF = ids.shape
    D = tables[0].shape[1]
    ND = dense_ctx.shape[1]
    H1 = w_top1.shape[1]
    H2 = w_top2.shape[1]
    T = 4
    MACRO = T * P
    NM = BATCH // MACRO
    NJ = NF - 1
    NPAIR = NF * NJ // 2
    KZ = NPAIR + ND + 1
    ZC = [(c, min(P, KZ - c)) for c in range(0, KZ, P)]
    ROW = 32
    S = P // ROW
    GT = P // S
    GB = 4
    NQ = GT // GB

    ONEHOT = [10, 15, 20, 11, 21, 18, 26]
    NO = len(ONEHOT)
    IDS_RUNS = [(0, 3), (3, 5), (5, 7)]
    VR = tables[ONEHOT[0]].shape[0]
    KT = 8
    RP = VR // KT
    HMASK = -(1 << 12)
    RING = 4
    UNIT = 4

    BATCHES = [[0, 1, 2, 3], [5, 6, 7, 8], [12, 13, 16, 17], [22, 23, 24, 25], [4, 9, 14, 19]]
    SLOT = {f: n for n, f in enumerate(f for b in BATCHES for f in b)}
    NG = len(SLOT)
    NB = len(BATCHES)

    ZB = [list(range(j, min(j + 4, NJ))) for j in range(0, NJ, 4)]
    NZ = len(ZB) + len(ZC)
    H1C = H1 // P
    H2C = H2 // P
    CHUNKS = ([[("turn", n) for n in range(b, min(b + 2, len(ZB)))] for b in range(0, len(ZB), 2)]
              + [[("pairs", 0), ("pairs", 1)], [("pairs", 2)]]
              + [[("hidden1", n)] for n in range(H1C)] + [[("hidden2", n)] for n in range(H2C)] + [[("score", 0)]])
    NH = H1C + H2C + 1

    OH = [("ids", 0), ("ids", 1)]
    for n in range(NO):
        OH += [("rows", n, k) for k in range(0, KT, UNIT)]
        if n + 2 < NO:
            OH.append(("ids", n + 2))
    OH_GROUPS = [OH[0:3]]
    for step in OH[3:]:
        if step[0] == "rows":
            OH_GROUPS.append([step])
        else:
            OH_GROUPS[-1].append(step)

    def interleave(first, second):
        steps = []
        for n in range(max(len(first), len(second))):
            steps += (first[n] if n < len(first) else []) + (second[n] if n < len(second) else [])
        return steps

    EARLY, GROUPS = OH[0:2], OH_GROUPS[:]
    GROUPS[0] = GROUPS[0][2:]
    TILES = [("tile", t) for t in range(T)]
    BODY = TILES[:-1] + EARLY + TILES[-1:] + interleave(CHUNKS, GROUPS)
    BODY_DVE = TILES + interleave(GROUPS, CHUNKS)
    LAST = TILES + [step for chunk in CHUNKS for step in chunk]

    class Phase:

        def __init__(self, steps, uses_before, fulls_before, per_macro=None):
            self.use, self.full = {}, {}
            uses = fulls = 0
            for step in steps:
                if step[0] == "tile":
                    self.use[step], self.full[step] = uses, fulls
                    uses, fulls = uses + NB, fulls + NB
                elif step[0] == "ids":
                    self.use[step], self.full[step] = uses, fulls
                    uses, fulls = uses + 1, fulls + 1
                elif step[0] == "rows" and step[2] == KT - UNIT:
                    self.use[("rows", step[1])] = uses
                    uses += 1
            self.uses, self.fulls = uses, fulls
            self.uses_before, self.fulls_before = uses_before, fulls_before
            self.repeats = per_macro

        def out(self, m, use):
            return self.uses_before + use + (self.uses * m if self.repeats else 0)

        def filled(self, m, full):
            return self.fulls_before + full + (self.fulls * m if self.repeats else 0)

    FIRST_P = Phase(OH, 0, 0)
    BODY_P = Phase(BODY, FIRST_P.uses, FIRST_P.fulls, True)
    LAST_P = Phase(LAST, FIRST_P.uses + BODY_P.uses * (NM - 1), FIRST_P.fulls + BODY_P.fulls * (NM - 1))
    assert FIRST_P.uses % 2 == 0 and BODY_P.uses % 2 == 0

    ctx = ExitStack()
    with ctx:
        def sb(name, shape, dt):
            return ctx.enter_context(nc.sbuf_tensor(name, shape, dt))

        def sem(name):
            return ctx.enter_context(nc.semaphore(name))

        ids_sb = sb("ids_sb", [P, NM, T, NF], i32)
        ids_now = sb("ids_now", [P, T, NF], i32)
        free = sb("free", [P, 6], fp32)
        ids16 = sb("ids16", [P, T, NO], fp16)
        idsb = sb("idsb", [P, 2, MACRO], fp16)
        rowid = sb("rowid", [P, KT], fp32)
        ident = sb("ident", [P, P], fp32)
        ident16 = sb("ident16", [P, P], fp16)
        emb = sb("emb", [P, T, NG, D], fp32)
        emb_t = sb("emb_t", [D, T, P, ROW], fp32)
        tab_hi = sb("tab_hi", [P, NO, KT, D], f32r)
        tab_lo = sb("tab_lo", [P, NO, KT, D], f32r)
        onehot = sb("onehot", [P, RING, MACRO], f32r)
        dots = sb("dots", [P, NJ * T * GT], fp32)
        dots_v = dots[:, :].rearrange("p (j g) -> p j g", j=NJ)
        z = sb("z", [P, S, KZ], fp32)
        z_t = sb("z_t", [P, len(ZC), MACRO], fp32)
        w1 = sb("w1", [P, len(ZC), H1], fp32)
        w2 = sb("w2", [P, H1C, H2], fp32)
        w3 = sb("w3", [P, H2C], fp32)
        b2 = sb("b2", [P, H2C], fp32)
        h1 = dots[:, 0:H1C * MACRO].rearrange("p (c n) -> p c n", c=H1C)
        h2 = z_t[:, 0:H2C, :]
        y = z_t[0:1, len(ZC) - 1, :]
        NRAW = 3
        raw = [dots[0:RP, n * KT * D:(n + 1) * KT * D] for n in range(NRAW)]
        high = [z[0:RP, :, :].rearrange("p s k -> p (s k)")[:, 0:KT * D],
                z_t[0:RP, :, :].rearrange("p s k -> p (s k)")[:, 0:KT * D]]

        turned = [ctx.enter_context(nc.psum_tensor(f"turned{n}", [P, 512], fp32)) for n in range(2)]
        dot_ps = [ctx.enter_context(nc.psum_tensor(f"dot_ps{n}", [P, 512], fp32)) for n in range(2)]
        z_ps = [ctx.enter_context(nc.psum_tensor(f"z_ps{n}", [P, 512], fp32)) for n in range(2)]
        h_ps = [ctx.enter_context(nc.psum_tensor(f"h_ps{n}", [P, 512], fp32)) for n in range(2)]

        ids_in = sem("ids_in")
        weights_in = sem("weights_in")
        dense_in = sem("dense_in")
        ones_done = sem("ones_done")
        raw_in = [sem(f"raw_in{n}") for n in range(NRAW)]
        masked = sem("masked")
        hi_done = sem("hi_done")
        lo_done = sem("lo_done")
        ident_zero = sem("ident_zero")
        ident_done = sem("ident_done")
        ident16_done = sem("ident16_done")
        rowid_done = sem("rowid_done")
        pads_done = sem("pads_done")
        ids16_done = sem("ids16_done")
        gathered = [[sem(f"gathered{t}_{b}") for b in range(NB)] for t in range(T)]
        tile_open = [sem(f"tile_open{t}") for t in range(T)]
        turned_full = sem("turned_full")
        turned_out = sem("turned_out")
        onehot_full = sem("onehot_full")
        onehot_used = sem("onehot_used")
        dot_full = sem("dot_full")
        dot_out = [sem("dot_out_dve"), sem("dot_out_act")]
        z_full = sem("z_full")
        z_out = sem("z_out")
        h_full = sem("h_full")
        h_out = sem("h_out")
        y_sent = sem("y_sent")

        FREE = 1
        DOT_FREE = 2

        block = ctx.enter_context(nc.Block())

        def batch_view(ap, feats):
            step = feats[1] - feats[0]
            if feats[-1] - feats[0] == step * (len(feats) - 1):
                return ap[:, feats[0]:feats[-1] + 1:step, :]
            jump = feats[2] - feats[0]
            return ap[:, feats[0]:feats[0] + 2 * jump, :].rearrange("d (a b) p -> d a b p", a=2)[:, :, 0:2, :]

        def own_dots(t, q, s):
            rows = slice(ROW * s, ROW * (s + 1))
            g0 = t * GT + q * GB
            return (dots_v[rows, :, g0:g0 + GB].rearrange("p j g -> p g j"),
                    dot_ps[q % 2][rows, 0:GB * S * NJ].rearrange("p (g c) -> p g c", g=GB)[:, :, s * NJ:(s + 1) * NJ])

        @block.sync
        def _(sp):
            sp.dma_start(ids_sb[:, :, :, :],
                         ids.rearrange("(m p t) f -> p m (t f)", m=NM, t=T).rearrange("p m (t f) -> p m t f", t=T)
                         ).then_inc(ids_in, 16)
            for n, f in enumerate(ONEHOT):
                if n >= NRAW:
                    sp.wait_ge(lo_done, n - NRAW + 1)
                for p0, p1 in ((0, RP // 16 * 16), (RP // 16 * 16, RP)):
                    sp.dma_start(raw[n % NRAW][p0:p1, :],
                                 tables[f].rearrange("(p k) d -> p (k d)", k=KT)[p0:p1, :]).then_inc(raw_in[n % NRAW], 16)
            sp.wait_ge(hi_done, NO)
            sp.wait_ge(lo_done, NO)
            for m in range(NM):
                sp.wait_ge(z_full, FREE + NZ * m)
                dense_v = dense_ctx[m * MACRO:(m + 1) * MACRO, :].rearrange("(g s t) c -> t g s c", s=S, t=T)
                for t in range(T):
                    sp.dma_start(z[t * GT:(t + 1) * GT, :, NPAIR:NPAIR + ND], dense_v[t]).then_inc(dense_in, 16)
                sp.wait_ge(h_out, FREE + NH * (m + 1))
                sp.dma_start(out[m * MACRO:(m + 1) * MACRO, :].rearrange("n o -> o n"), y[:, :]).then_inc(y_sent, 16)
            sp.wait_ge(y_sent, 16 * (NM + 1))

        @block.gpsimd
        def _(pool):
            nc.gpsimd.iota(rowid[0:RP, :], [[1, KT]], base=0, channel_multiplier=KT,
                           allow_small_or_imprecise_dtypes=True).then_inc(rowid_done, 1)
            pool.wait_ge(ident_zero, 1)
            nc.gpsimd.affine_select(out=ident[:, :], in_=ident[:, :], compare_op=ALU.not_equal, fill=1.0, base=0,
                                    pattern=[[-1, P]], channel_multiplier=1).then_inc(ident_done, 1)
            with pool.Fori(1, NM + 1) as opened:
                for t in range(T):
                    pool.wait_ge(ids_in, 16)
                    pool.wait_ge(tile_open[t], opened)
                    for b, feats in enumerate(BATCHES):
                        for f in feats:
                            nc.gpsimd.indirect_dma_start(
                                out=emb[:, t, SLOT[f], :], out_offset=None, in_=tables[f],
                                in_offset=bass.IndirectOffsetOnAxis(ap=ids_now[:, t, f:f + 1], axis=0),
                            ).then_inc(gathered[t][b], 16)

        @block.tensor
        def _(pe):
            def onehot_step(ph, m, mo, step):
                if step[0] == "ids":
                    _, n = step
                    use = ph.use[step]
                    if n == 0:
                        pe.wait_ge(ids16_done, mo + 1)
                    if ph.out(0, use) >= 2:
                        pe.wait_ge(turned_out, ph.out(m, use) - 1)
                    bank = turned[use % 2]
                    for t in range(T):
                        last = nc.tensor.matmul(bank[:, t * P:(t + 1) * P],
                                                ids16[:, t, n:n + 1].to_broadcast([P, P]), ident16[:, :],
                                                start=True, stop=True)
                    last.then_inc(turned_full, 1)
                    return
                _, n, k0 = step
                use = ph.use[("rows", n)]
                bank = turned[use % 2]
                if k0 == 0:
                    if ph is FIRST_P:
                        pe.wait_ge(hi_done, n + 1)
                        pe.wait_ge(lo_done, n + 1)
                    pe.wait_ge(turned_out, ph.out(m, use) - 1)
                for k in range(k0, k0 + UNIT):
                    at = KT * n + k
                    pe.wait_ge(onehot_full, NO * KT * mo + at + 1)
                    nc.tensor.matmul(bank[:, :], tab_hi[0:RP, n, k, :], onehot[0:RP, at % RING, :],
                                     start=(k == 0), stop=False)
                    last = nc.tensor.matmul(bank[:, :], tab_lo[0:RP, n, k, :], onehot[0:RP, at % RING, :],
                                            start=False, stop=(k == KT - 1))
                    last.then_inc(onehot_used, 1)

            def tile(ph, m, t):
                for b, feats in enumerate(BATCHES):
                    use = ph.use[("tile", t)] + b
                    pe.wait_ge(gathered[t][b], 16 * len(feats) * (m + 1))
                    pe.wait_ge(turned_out, ph.out(m, use) - 1)
                    for q, f in enumerate(feats):
                        last = nc.tensor.transpose(turned[use % 2][:, q * P:(q + 1) * P], emb[:, t, SLOT[f], :],
                                                   ident[:, :])
                    last.then_inc(turned_full, 1)
                pe.wait_ge(turned_out, ph.out(m, ph.use[("tile", t)] + NB))
                for q in range(NQ):
                    bank = dot_ps[q % 2]
                    for n in range(2):
                        pe.wait_ge(dot_out[n], DOT_FREE + T * NQ * m + NQ * t + q - 1)
                    for g in range(GB):
                        four = emb_t[:, t, (q * GB + g) * S:(q * GB + g + 1) * S, :]
                        last = nc.tensor.matmul(bank[:, g * S * NJ:(g + 1) * S * NJ].rearrange("p (s j) -> p s j", j=NJ),
                                                four.rearrange("d s f -> d (s f)"), four[:, :, 1:NF], start=True, stop=True)
                    last.then_inc(dot_full, 1)

            def mlp_step(m, step):
                kind, n = step
                if kind in ("turn", "pairs"):
                    use = n if kind == "turn" else len(ZB) + n
                    bank = z_ps[use % 2]
                    if step == ("turn", 0):
                        for half in range(2):
                            pe.wait_ge(dot_out[half], DOT_FREE + T * NQ * (m + 1))
                    if step == ("pairs", 0):
                        pe.wait_ge(z_out, FREE + NZ * m + len(ZB))
                        pe.wait_ge(dense_in, 16 * T * (m + 1))
                    pe.wait_ge(z_out, FREE + NZ * m + max(use - 1, 0))
                    if kind == "turn":
                        for q, j in enumerate(ZB[n]):
                            last = nc.tensor.transpose(bank[:, q * P:(q + 1) * P], dots_v[:, j, :], ident[:, :])
                    else:
                        c, w = ZC[n]
                        for s in range(S):
                            last = nc.tensor.transpose(bank[0:w, s * P:(s + 1) * P], z[:, s, c:c + w], ident[:, :])
                    last.then_inc(z_full, 1)
                    return
                use = {"hidden1": 0, "hidden2": H1C, "score": H1C + H2C}[kind] + n
                bank = h_ps[use % 2]
                if step == ("hidden1", 0):
                    pe.wait_ge(z_out, FREE + NZ * (m + 1))
                before = {"hidden1": max(n - 1, 0), "hidden2": H1C, "score": H1C + H2C}[kind]
                pe.wait_ge(h_out, FREE + NH * m + before)
                if kind == "hidden1":
                    for c, (_, w) in enumerate(ZC):
                        last = nc.tensor.matmul(bank[:, :], w1[0:w, c, n * P:(n + 1) * P], z_t[0:w, c, :],
                                                start=(c == 0), stop=(c == len(ZC) - 1))
                elif kind == "hidden2":
                    for c in range(H1C):
                        last = nc.tensor.matmul(bank[:, :], w2[:, c, n * P:(n + 1) * P], h1[:, c, :],
                                                start=(c == 0), stop=(c == H1C - 1))
                else:
                    for c in range(H2C):
                        last = nc.tensor.matmul(bank[0:1, :], w3[:, c:c + 1], h2[:, c, :],
                                                start=(c == 0), stop=(c == H2C - 1))
                last.then_inc(h_full, 1)

            def run(ph, m, steps):
                for step in steps:
                    if step[0] == "tile":
                        tile(ph, m, step[1])
                    elif step[0] in ("ids", "rows"):
                        onehot_step(ph, m, 0 if ph is FIRST_P else m + 1, step)
                    else:
                        mlp_step(m, step)

            pe.wait_ge(ident16_done, 1)
            run(FIRST_P, 0, OH)
            pe.wait_ge(ident_done, 1)
            pe.wait_ge(pads_done, 1)
            pe.wait_ge(weights_in, 16 * 7)
            pe.wait_ge(ones_done, 1)
            with pe.Fori(0, NM - 1) as m:
                run(BODY_P, m, BODY)
            run(LAST_P, NM - 1, LAST)

        @block.scalar
        def _(act):
            for c, (c0, w) in enumerate(ZC):
                rows = min(w, NPAIR + ND - c0)
                act.dma_start(w1[0:rows, c, :], w_top1[c0:c0 + rows, :]).then_inc(weights_in, 16)
            act.dma_start(w1[ZC[-1][1] - 1:ZC[-1][1], len(ZC) - 1, :],
                          b_top1.rearrange("(o h) -> o h", o=1)).then_inc(weights_in, 16)
            act.dma_start(w2[:, :, :], w_top2.rearrange("(c p) h -> p c h", p=P)).then_inc(weights_in, 16)
            with nc.allow_non_contiguous_dma(reason="256 single words, once"):
                act.dma_start(w3[:, :], w_top3.rearrange("(c p) o -> p (c o)", p=P)).then_inc(weights_in, 16)
                act.dma_start(b2[:, :], b_top2.rearrange("(c p) -> p c", p=P)).then_inc(weights_in, 16)
            def onehot_step(ph, m, mo, step):
                _, n = step[0:2]
                if step[0] == "ids":
                    act.wait_ge(turned_full, ph.filled(m, ph.full[step] + 1))
                    if ph is not FIRST_P or n >= 2:
                        act.wait_ge(onehot_full, KT * (NO * mo + max(n - 1, 0)))
                    nc.scalar.copy(idsb[:, n % 2, :], turned[ph.use[step] % 2][:, :]).then_inc(turned_out, 1)
                elif step[2] + UNIT == KT:
                    act.wait_ge(onehot_used, KT * (NO * mo + n + 1))
                    f = ONEHOT[n]
                    nc.scalar.copy(emb_t[:, :, :, f],
                                   turned[ph.use[("rows", n)] % 2][:, :].rearrange("d (t p) -> d t p", t=T)
                                   ).then_inc(turned_out, 1)

            def tile(ph, m, t):
                for b, feats in enumerate(BATCHES):
                    act.wait_ge(turned_full, ph.filled(m, ph.full[("tile", t)] + b + 1))
                    dst = batch_view(emb_t[:, t, :, :].rearrange("d p f -> d f p"), feats)
                    src = turned[(ph.use[("tile", t)] + b) % 2][:, 0:len(feats) * P]
                    if len(dst.shape) == 4:
                        src = src.rearrange("d (a b p) -> d a b p", a=2, b=2)
                    else:
                        src = src.rearrange("d (q p) -> d q p", p=P)
                    nc.scalar.copy(dst, src).then_inc(turned_out, 1)
                for q in range(NQ):
                    act.wait_ge(dot_full, T * NQ * m + NQ * t + q + 1)
                    for s in (2, 3):
                        dst, src = own_dots(t, q, s)
                        last = nc.scalar.copy(dst, src)
                    last.then_inc(dot_out[1], 1)

            def mlp_step(m, step):
                kind, n = step
                if kind not in ("hidden1", "hidden2", "score"):
                    return
                use = {"hidden1": 0, "hidden2": H1C, "score": H1C + H2C}[kind] + n
                bank = h_ps[use % 2]
                act.wait_ge(h_full, NH * m + use + 1)
                if kind == "hidden1":
                    nc.scalar.activation(h1[:, n, :], bank[:, :], ACT.Relu).then_inc(h_out, 1)
                elif kind == "hidden2":
                    nc.scalar.activation(h2[:, n, :], bank[:, :], ACT.Relu, bias=b2[:, n:n + 1]).then_inc(h_out, 1)
                else:
                    nc.scalar.copy(y[:, :].rearrange("o (g s t) -> o s t g", s=S, t=T),
                                   bank[0:1, :].rearrange("o (s t g) -> o s t g", s=S, t=T)).then_inc(h_out, 1)

            def table_high(n):
                act.wait_ge(masked, n + 1)
                nc.scalar.copy(tab_hi[0:RP, n, :, :], high[n % 2].rearrange("p (k d) -> p k d", k=KT)
                               ).then_inc(hi_done, 1)

            def run(ph, m, steps):
                for step in steps:
                    if step[0] == "tile":
                        tile(ph, m, step[1])
                    elif step[0] in ("ids", "rows"):
                        onehot_step(ph, m, 0 if ph is FIRST_P else m + 1, step)
                    else:
                        mlp_step(m, step)

            for n in range(2):
                table_high(n)
            for step in OH:
                if step[0] == "rows" and step[2] == 0 and step[1] + 2 < NO:
                    table_high(step[1] + 2)
                run(FIRST_P, 0, [step])
            act.wait_ge(weights_in, 16 * 7)
            with act.Fori(0, NM - 1) as m:
                run(BODY_P, m, BODY)
            run(LAST_P, NM - 1, LAST)

        @block.vector
        def _(dve):
            def ids_to_fp16(m):
                for n0, n1 in IDS_RUNS:
                    f0, f1 = ONEHOT[n0], ONEHOT[n1 - 1]
                    last = nc.vector.tensor_copy(
                        ids16[:, :, n0:n1],
                        ids_sb[:, bass.ds(m, 1), :, f0:f1 + 1:ONEHOT[n0 + 1] - f0].rearrange("p m t f -> p (m t) f"))
                last.then_inc(ids16_done, 1)

            def onehot_step(ph, m, mo, step):
                if step[0] == "ids":
                    return
                _, n, k0 = step
                if k0 == 0:
                    dve.wait_ge(turned_out, ph.out(m, ph.use[("ids", n)] + 1))
                for k in range(k0, k0 + UNIT):
                    at = KT * n + k
                    if ph is not FIRST_P or at >= RING:
                        dve.wait_ge(onehot_used, NO * KT * mo + at - RING + 1)
                    nc.vector.tensor_scalar(onehot[0:RP, at % RING, :], idsb[0:RP, n % 2, :], rowid[0:RP, k:k + 1],
                                            None, ALU.is_equal).then_inc(onehot_full, 1)

            def open_tile(m, t):
                nc.vector.tensor_copy(ids_now[:, t, :], ids_sb[:, bass.ds(m, 1), t, :].rearrange("p m f -> p (m f)")
                                      ).then_inc(tile_open[t], 1)

            def tile(m, t):
                for q in range(NQ):
                    dve.wait_ge(dot_full, T * NQ * m + NQ * t + q + 1)
                    for s in (0, 1):
                        dst, src = own_dots(t, q, s)
                        last = nc.vector.tensor_copy(dst, src)
                    last.then_inc(dot_out[0], 1)
                    if q == 0 and not isinstance(m, int):
                        open_tile(m + 1, t)

            def mlp_step(m, step):
                kind, n = step
                if kind == "turn":
                    dve.wait_ge(z_full, FREE + NZ * m + n + 1)
                    for q, j in enumerate(ZB[n]):
                        off = j * (j + 1) // 2
                        last = nc.vector.tensor_copy(
                            z[:, :, off:off + j + 1],
                            z_ps[n % 2][:, q * P:(q + 1) * P].rearrange("g (s i) -> g s i", s=S)[:, :, 0:j + 1])
                    last.then_inc(z_out, 1)
                elif kind == "pairs":
                    use = len(ZB) + n
                    w = ZC[n][1]
                    if n == len(ZC) - 1:
                        dve.wait_ge(y_sent, 16 * (m + 1))
                    dve.wait_ge(z_full, FREE + NZ * m + use + 1)
                    nc.vector.tensor_copy(z_t[0:w, n, :], z_ps[use % 2][0:w, :]).then_inc(z_out, 1)

            nc.vector.memset(ident[:, :], 0.0).then_inc(ident_zero, 1)
            nc.vector.memset(free[:, 0:1], 0.0).then_inc(dot_out[0], DOT_FREE)
            nc.vector.memset(free[:, 4:5], 0.0).then_inc(dot_out[1], DOT_FREE)
            nc.vector.memset(free[:, 1:2], 0.0).then_inc(z_out, FREE)
            nc.vector.memset(free[:, 5:6], 0.0).then_inc(z_full, FREE)
            nc.vector.memset(free[:, 2:3], 0.0).then_inc(h_out, FREE)
            nc.vector.memset(free[:, 3:4], 0.0).then_inc(y_sent, 16)
            nc.vector.memset(emb_t[:, :, :, NF:ROW], 0.0).then_inc(pads_done, 1)
            dve.wait_ge(ids_in, 16)
            for t in range(T):
                open_tile(0, t)
            ids_to_fp16(0)
            dve.wait_ge(ident_done, 1)
            nc.vector.tensor_copy(ident16[:, :], ident[:, :]).then_inc(ident16_done, 1)
            dve.wait_ge(rowid_done, 1)

            def table_mask(n):
                dve.wait_ge(raw_in[n % NRAW], 32 * (n // NRAW + 1))
                if n >= 2:
                    dve.wait_ge(hi_done, n - 1)
                    dve.wait_ge(lo_done, n - 1)
                nc.vector.tensor_scalar(high[n % 2].bitcast(i32), raw[n % NRAW].bitcast(i32), HMASK, None,
                                        ALU.bitwise_and).then_inc(masked, 1)

            def table_low(n):
                dve.wait_ge(masked, n + 1)
                nc.vector.tensor_tensor(tab_lo[0:RP, n, :, :].rearrange("p k d -> p (k d)"), raw[n % NRAW],
                                        high[n % 2], ALU.subtract).then_inc(lo_done, 1)

            table_mask(0)
            table_mask(1)
            for step in OH:
                if step[0] == "rows" and step[2] == 0:
                    table_low(step[1])
                elif step[0] == "rows" and step[2] == UNIT and step[1] + 2 < NO:
                    table_mask(step[1] + 2)
                onehot_step(FIRST_P, 0, 0, step)
            dve.wait_ge(hi_done, NO)
            dve.wait_ge(lo_done, NO)
            nc.vector.memset(z[:, :, KZ - 1:KZ], 1.0).then_inc(ones_done, 1)

            def run(ph, m, steps):
                for step in steps:
                    if step[0] == "tile":
                        tile(m, step[1])
                    elif step[0] in ("ids", "rows"):
                        onehot_step(ph, m, m + 1, step)
                    else:
                        mlp_step(m, step)

            with dve.Fori(0, NM - 1) as m:
                ids_to_fp16(m + 1)
                run(BODY_P, m, BODY_DVE)
            run(LAST_P, NM - 1, LAST)


_INS = ["dense_ctx", "ids"] + [f"tbl_{i}" for i in range(27)] + ["W_top1", "b_top1", "W_top2", "b_top2", "W_top3"]


def kernel(**inputs):
    import numpy as _np
    import concourse.bacc as _bacc
    from concourse import mybir as _mybir
    from concourse.bass_utils import run_bass_kernel_spmd as _run

    nc = _bacc.Bacc("TRN2", target_bir_lowering=False, num_devices=1)
    arrays, args = {}, {}
    for name in _INS:
        a = _np.ascontiguousarray(inputs[name])
        arrays[f"in_{name}_dram"] = a
        args[name] = nc.dram_tensor(f"in_{name}_dram", a.shape, _mybir.dt.from_np(a.dtype), kind="ExternalInput").ap()
    batch = inputs["ids"].shape[0]
    out = nc.dram_tensor("out_0_dram", (batch, 1), _mybir.dt.float32, kind="ExternalOutput").ap()
    dlrm_tower(nc, args["dense_ctx"], args["ids"], [args[f"tbl_{i}"] for i in range(27)],
               args["W_top1"], args["b_top1"], args["W_top2"], args["b_top2"], args["W_top3"], out)
    r = _run(nc, [arrays], core_ids=[0])
    return r.results[0]["out_0_dram"]
```

```python
import concourse.bass as bass
from concourse import mybir
from contextlib import ExitStack


def dlrm_tower(nc, dense_ctx, ids, tables, w_top1, b_top1, w_top2, b_top2, w_top3, out):
    fp32 = mybir.dt.float32
    f32r = mybir.dt.float32r
    fp16 = mybir.dt.float16
    i32 = mybir.dt.int32
    ALU = mybir.AluOpType
    ACT = mybir.ActivationFunctionType

    P = 128
    BATCH, NF = ids.shape
    D = tables[0].shape[1]
    ND = dense_ctx.shape[1]
    H1 = w_top1.shape[1]
    H2 = w_top2.shape[1]
    T = 4
    MACRO = T * P
    HALF = MACRO // 2
    NM = BATCH // MACRO
    NJ = NF - 1
    NPAIR = NF * NJ // 2
    KZ = NPAIR + ND + 1
    ZC = [(c, min(P, KZ - c)) for c in range(0, KZ, P)]
    ROW = 32
    S = P // ROW
    GT = P // S
    GB = 4
    NQ = GT // GB

    ONEHOT = [10, 15, 20, 11, 21, 18, 26]
    IDS_RUNS = [(0, 3), (3, 5), (5, 7)]
    NO = len(ONEHOT)
    KT = 8
    RP = tables[ONEHOT[0]].shape[0] // KT

    BATCHES = [[0, 1, 2, 3], [5, 6, 7, 8], [12, 13, 16, 17], [22, 23, 24, 25], [4, 9, 14, 19]]
    SLOT = {f: n for n, f in enumerate(f for b in BATCHES for f in b)}
    NG = len(SLOT)
    NB = len(BATCHES)
    NS = 2

    ZB = [list(range(j, min(j + 4, NJ))) for j in range(0, NJ, 4)]
    NTURN = [len(ZB[0::2]), len(ZB[1::2])]
    H1C = H1 // P
    H2C = H2 // P
    NH = H2C + 1

    U = 2 * NO
    U0 = NO + NO // 2

    def mlp_steps(h):
        return ([[("pairs", h, 0), ("pairs", h, 1)], [("pairs", h, 2)]]
                + [[("hidden1", h, n), ("hidden1", h, n + 1)] for n in range(0, H1C, 2)]
                + [[("hidden2", h, n) for n in range(H2C)], [("score", h)]])

    halves = [mlp_steps(0), mlp_steps(1)]
    both = halves[0] + halves[1]
    MLP = [both[0:4], both[4:8], both[8:12]]
    TURN = [[("turn", n) for n in range(b, min(b + 2, len(ZB)))] for b in range(0, len(ZB), 2)]

    def stretch(units, others, rows):
        units, others, rows = list(units), list(others), list(rows)
        steps = []
        for kind in "OXOXRRXORRX":
            if kind == "O" and len(units) > 1:
                u = units.pop(0)
                steps += [("onehot", u), ("ids", u + 2)]
            if kind == "X" and others:
                steps += others.pop(0)
            if kind == "R" and rows:
                steps.append(rows.pop(0))
        steps += rows
        for u in units:
            steps += [("onehot", u), ("ids", u + 2)]
        return steps

    def macro_steps(mlp_before, after):
        steps = []
        for t in range(T):
            steps += [("dots", t, q) for q in range(NQ)]
            units = range(U0 + t * U // T, U0 + (t + 1) * U // T)
            last = 2 * U if after else U
            others = TURN if t == T - 1 else (MLP[t] if mlp_before else [])
            rows = [("rows", t + 1, b) for b in range(NB)] if t + 1 < T or after else []
            steps += [x for x in stretch([u for u in units if u < last], others, rows)
                      if x[0] != "ids" or x[1] < last]
        return steps

    class Phase:

        def __init__(self, steps, before=None):
            self.steps, self.before = steps, before
            self.use, self.full = {}, {}
            for step in steps:
                if step[0] in ("rows", "onehot"):
                    if step[0] == "rows":
                        self.full[step] = len(self.full)
                    self.use[step] = len(self.use)

        def first_use(self, m):
            return len(PRO.use) + len(FIRST.use) * m if self is not PRO else 0

        def bank(self, step):
            return (self.first_use(0) + self.use[step]) % 2

        def free(self, m, step):
            return self.first_use(m) + self.use[step] - 1

        def filled(self, m, step):
            first = len(PRO.full) + len(FIRST.full) * m if self is not PRO else 0
            return first + self.full[step] + 1

        def tile_out(self, m, t):
            if t == 0:
                last = max(self.before.use[("rows", T, NB - 1)], self.before.use[("onehot", U + NO - 1)])
                return self.first_use(m) - len(self.before.use) + last + 1
            last = self.use[("rows", t, NB - 1)]
            if t == 2:
                last = max(last, self.use[("onehot", U - 1)])
            return self.first_use(m) + last + 1

        def for_dve(self):
            steps = [("columns", U)] if self is PRO else [("ids16", 0)]
            for step in self.steps:
                if step[0] == "onehot":
                    if self is not LAST or step[1] + 1 < U:
                        steps.append(("columns", step[1] + 1))
                elif step == ("dots", 1, NQ - 1):
                    steps += [step, ("ids16", 1)]
                elif step[0] != "ids" and step[0] != "rows":
                    steps.append(step)
            return [x for x in steps if x[0] != "ids16" or self is not LAST]

    pro = [("ids", U), ("ids", U + 1)]
    for n in range(U0):
        pro += [("onehot", U + n), ("ids", U + n + 2)]
        if U0 - n <= NB:
            pro.append(("rows", T, NB - U0 + n))
    PRO = Phase(pro)
    FIRST = Phase(macro_steps(False, True), PRO)
    BODY = Phase(macro_steps(True, True), FIRST)
    last_steps = macro_steps(True, False)
    for step, before in ((("onehot", U - 1), ("rows", 2, 0)),
                         (("score", 0), ("rows", 2, NB - 1)),
                         (("pairs", 1, 0), ("dots", 2, 0)),
                         (("pairs", 1, 1), ("dots", 2, 0)),
                         (("pairs", 1, 2), ("dots", 2, 0)),
                         (("hidden2", 1, 1), ("rows", 3, NB - 1)),
                         (("score", 1), ("dots", 3, 0))):
        last_steps.remove(step)
        last_steps.insert(last_steps.index(before), step)
    LAST = Phase(last_steps, BODY)
    A, B = [[x for chunk in half for x in chunk] for half in halves]
    TAIL = B[0:2] + A[0:1] + B[2:3] + A[1:3] + [step for pair in zip(B[3:], A[3:]) for step in pair]
    assert len(FIRST.use) == len(BODY.use) and len(FIRST.use) % 2 == 0 and len(FIRST.full) == len(BODY.full)

    ctx = ExitStack()
    with ctx:
        def sb(name, shape, dt):
            return ctx.enter_context(nc.sbuf_tensor(name, shape, dt))

        def sem(name):
            return ctx.enter_context(nc.semaphore(name))

        ids_sb = sb("ids_sb", [P, NM * T, NF], i32)
        ids_now = sb("ids_now", [P, NS, NF], i32)
        ids16 = sb("ids16", [P, T, NO], fp16)
        idsb = sb("idsb", [P, 2, HALF], fp16)
        rowid = sb("rowid", [P, KT], fp32)
        ident = sb("ident", [P, P], fp32)
        ident16 = sb("ident16", [P, P], fp16)
        emb = sb("emb", [P, NS, NG, D], fp32)
        emb_t = sb("emb_t", [D, T, P, ROW], fp32)
        tab_hi = sb("tab_hi", [P, NO, KT, D], f32r)
        tab_lo = sb("tab_lo", [P, NO, KT, D], f32r)
        onehot = sb("onehot", [P, KT, HALF], f32r)
        dots = sb("dots", [P, NJ * T * GT], fp32)
        dots_v = dots[:, :].rearrange("p (j g) -> p j g", j=NJ)
        z = sb("z", [P, S, KZ], fp32)
        z_hi = sb("z_hi", [P, len(ZC), HALF], f32r)
        z_lo = sb("z_lo", [P, len(ZC), HALF], f32r)
        h1_hi = sb("h1_hi", [P, H1C, HALF], f32r)
        h1_lo = sb("h1_lo", [P, H1C, HALF], f32r)
        w1_hi = sb("w1_hi", [P, len(ZC), H1], f32r)
        w1_lo = sb("w1_lo", [P, len(ZC), H1], f32r)
        w2_hi = sb("w2_hi", [P, H1C, H2], f32r)
        w2_lo = sb("w2_lo", [P, H1C, H2], f32r)
        h2 = sb("h2", [P, H2C, HALF], fp32)
        w3 = sb("w3", [P, H2C], fp32)
        b2 = sb("b2", [P, H2C], fp32)
        start = sb("start", [P, 2], fp32)
        z_flat = z[:, :, :].rearrange("p s k -> p (s k)")
        W_PARTS = [(P, z_flat[:, 0:2 * H1], w1_hi[:, 0:2, :], w1_lo[:, 0:2, :]),
                   (ZC[2][1], z_flat[:, 0:H1], w1_hi[:, 2, :], w1_lo[:, 2, :]),
                   (P, z_flat[:, 0:H1C * H2], w2_hi[:, :, :], w2_lo[:, :, :])]
        W_COUNT = [16, 48, 64]
        NRAW = 3
        raw = [dots[0:RP, n * KT * D:(n + 1) * KT * D] for n in range(NRAW)]

        turned = [ctx.enter_context(nc.psum_tensor(f"turned{n}", [P, 512], fp32)) for n in range(2)]
        dot_ps = [ctx.enter_context(nc.psum_tensor(f"dot_ps{n}", [P, 512], fp32)) for n in range(2)]
        z_ps = [ctx.enter_context(nc.psum_tensor(f"z_ps{n}", [P, 512], fp32)) for n in range(2)]
        ids_ps = ctx.enter_context(nc.psum_tensor("ids_ps", [P, HALF], fp32))
        h_ps0 = ctx.enter_context(nc.psum_tensor("h_ps", [P, 512], fp32))

        ids_in = sem("ids_in")
        ids_rest_in = sem("ids_rest_in")
        weights_in = sem("weights_in")
        dense_in = sem("dense_in")
        w_raw_in = sem("w_raw_in")
        w_hi_done = sem("w_hi_done")
        w_lo_done = sem("w_lo_done")
        raw_in = [sem(f"raw_in{n}") for n in range(NRAW)]
        hi_done = sem("hi_done")
        lo_done = sem("lo_done")
        ident_zero = sem("ident_zero")
        ident_done = sem("ident_done")
        ident16_done = sem("ident16_done")
        rowid_done = sem("rowid_done")
        pads_done = sem("pads_done")
        ones_done = sem("ones_done")
        ids16_done = sem("ids16_done")
        tile_open = [sem(f"tile_open{n}") for n in range(NS)]
        gathered = [[sem(f"gathered{n}_{b}") for b in range(NB)] for n in range(NS)]
        rows_full = sem("rows_full")
        ids_full = sem("ids_full")
        ids_out = sem("ids_out")
        turned_out = sem("turned_out")
        onehot_full = sem("onehot_full")
        onehot_used = sem("onehot_used")
        dot_full = sem("dot_full")
        dot_out = [sem("dot_out_dve"), sem("dot_out_act")]
        turn_full = sem("turn_full")
        turn_out = [sem("turn_out_dve"), sem("turn_out_act")]

        class Side:

            def __init__(self, name, z_hi, z_lo, h1_hi, h1_lo, h2, z_ps, h_ps, h_start):
                self.z_hi, self.z_lo, self.h1_hi, self.h1_lo, self.h2 = z_hi, z_lo, h1_hi, h1_lo, h2
                self.z_ps, self.h_ps = z_ps, h_ps
                self.pairs_full = sem("pairs_full" + name)
                self.z_hi_out = sem("z_hi_out" + name)
                self.z_lo_out = sem("z_lo_out" + name)
                self.h_full = sem("h_full" + name)
                self.h1_hi_out = sem("h1_hi_out" + name)
                self.h1_lo_out = sem("h1_lo_out" + name)
                self.h_out = sem("h_out" + name)
                self.y_sent = sem("y_sent" + name)
                self.h_start = h_start
                self.y = h2[0:1, 0, :]

        main = Side("", z_hi, z_lo, h1_hi, h1_lo, h2, z_ps, [h_ps0, z_ps[1]], 1)
        tab_flat = tab_hi[:, :, :, :].rearrange("p n k d -> p (n k d)")
        bounds = [0]
        for chunks in (len(ZC), len(ZC), H1C, H1C):
            bounds.append(bounds[-1] + chunks * HALF)
        late = Side("_late", *[tab_flat[:, a:b].rearrange("p (c n) -> p c n", n=HALF) for a, b in zip(bounds, bounds[1:])],
                    emb[:, :, :, :].rearrange("p n g d -> p (n g d)")[:, 0:H2C * HALF].rearrange("p (c n) -> p c n", n=HALF),
                    dot_ps, turned, 0)

        block = ctx.enter_context(nc.Block())

        def wait(engine, semaphore, count):
            if not isinstance(count, int) or count > 0:
                engine.wait_ge(semaphore, count)

        def hidden_use(step):
            return {"hidden1": 0, "hidden2": H1C, "score": H1C + H2C}[step[0]] + (step[2] if len(step) > 2 else 0)

        def turn_bank(ph, n):
            banks = z_ps + turned if ph is LAST else z_ps
            return banks[n % len(banks)], len(banks)

        TURNS_BEFORE = []
        for c, w in ZC:
            need = [n for n, js in enumerate(ZB) if js[0] * (js[0] + 1) // 2 < c + w]
            TURNS_BEFORE.append([sum(n % 2 == k for n in need) for k in range(2)])

        def side_of_tail(step):
            return (main, 2 * (NM - 1)) if step[1] == 0 else (late, 0)

        NU = H1C + H2C + 1

        def batch_view(ap, feats):
            step = feats[1] - feats[0]
            if feats[-1] - feats[0] == step * (len(feats) - 1):
                return ap[:, feats[0]:feats[-1] + 1:step, :]
            jump = feats[2] - feats[0]
            return ap[:, feats[0]:feats[0] + 2 * jump, :].rearrange("d (a b) p -> d a b p", a=2)[:, :, 0:2, :]

        def own_dots(t, q, s):
            rows = slice(ROW * s, ROW * (s + 1))
            g0 = t * GT + q * GB
            return (dots_v[rows, :, g0:g0 + GB].rearrange("p j g -> p g j"),
                    dot_ps[q % 2][rows, 0:GB * S * NJ].rearrange("p (g c) -> p g c", g=GB)[:, :, s * NJ:(s + 1) * NJ])

        def turned_dots_out(engine, copy, ph, m, step):
            n = step[1]
            engine.wait_ge(turn_full, len(ZB) * m + n + 1)
            for q, j in enumerate(ZB[n]):
                off = j * (j + 1) // 2
                last = copy(z[:, :, off:off + j + 1],
                            turn_bank(ph, n)[0][:, q * P:(q + 1) * P].rearrange("g (s i) -> g s i", s=S)[:, :, 0:j + 1])
            last.then_inc(turn_out[n % 2], 1)

        @block.sync
        def _(sp):
            def load_ids(m0, m1, semaphore):
                sp.dma_start(ids_sb[:, :, :].rearrange("p (m t) f -> p m (t f)", t=T)[:, m0:m1, :],
                             ids.rearrange("(m p t) f -> p m (t f)", m=NM, t=T)[:, m0:m1, :]).then_inc(semaphore, 16)

            load_ids(0, 1, ids_in)
            for n, f in enumerate(ONEHOT):
                wait(sp, lo_done, n - NRAW + 1)
                for p0, p1 in ((0, RP // 16 * 16), (RP // 16 * 16, RP)):
                    sp.dma_start(raw[n % NRAW][p0:p1, :],
                                 tables[f].rearrange("(p k) d -> p (k d)", k=KT)[p0:p1, :]).then_inc(raw_in[n % NRAW], 16)
            load_ids(1, NM, ids_rest_in)
            full, rest = 2 * P, NPAIR + ND - 2 * P
            sp.dma_start(z_flat[:, 0:2 * H1].rearrange("p (c h) -> p c h", c=2),
                         w_top1[0:full, :].rearrange("(c p) h -> p c h", p=P)).then_inc(w_raw_in, 16)
            sp.wait_ge(w_lo_done, 1)
            sp.dma_start(z_flat[0:rest, 0:H1], w_top1[full:full + rest, :]).then_inc(w_raw_in, 16)
            sp.dma_start(z_flat[rest:rest + 1, 0:H1], b_top1.rearrange("(o h) -> o h", o=1)).then_inc(w_raw_in, 16)
            sp.wait_ge(w_lo_done, 2)
            sp.dma_start(z_flat[:, 0:H1C * H2].rearrange("p (c h) -> p c h", c=H1C),
                         w_top2.rearrange("(c p) h -> p c h", p=P)).then_inc(w_raw_in, 16)
            sp.wait_ge(w_lo_done, 3)
            dense_v = dense_ctx.rearrange("(m g s t) c -> m t g s c", m=NM, s=S, t=T)

            def dense(m):
                wait(sp, main.pairs_full, 2 * len(ZC) * m)
                for t in range(T):
                    sp.dma_start(z[t * GT:(t + 1) * GT, :, NPAIR:NPAIR + ND], dense_v[m, t]).then_inc(dense_in, 16)

            dense(0)
            def send(m, h, side, half):
                sp.wait_ge(side.h_out, side.h_start + NH * (half + 1))
                sp.dma_start(out.rearrange("(m g h r) o -> m h o g r", m=NM, g=GT, h=2)[m, h],
                             side.y.rearrange("o (g r) -> o g r", g=GT)).then_inc(side.y_sent, 16)

            for m in range(NM - 1):
                dense(m + 1)
                for h in range(2):
                    send(m, h, main, 2 * m + h)
            send(NM - 1, 0, main, 2 * (NM - 1))
            send(NM - 1, 1, late, 0)
            sp.wait_ge(main.y_sent, 16 * 2 * NM)
            sp.wait_ge(late.y_sent, 16)

        @block.gpsimd
        def _(pool):
            nc.gpsimd.iota(rowid[0:RP, :], [[1, KT]], base=0, channel_multiplier=KT,
                           allow_small_or_imprecise_dtypes=True).then_inc(rowid_done, 1)
            pool.wait_ge(ident_zero, 1)
            nc.gpsimd.affine_select(out=ident[:, :], in_=ident[:, :], compare_op=ALU.not_equal, fill=1.0, base=0,
                                    pattern=[[-1, P]], channel_multiplier=1).then_inc(ident_done, 1)
            with pool.Fori(1, NM * T // NS + 1) as opened:
                for slot in range(NS):
                    pool.wait_ge(ids_in, 16)
                    pool.wait_ge(tile_open[slot], opened)
                    for b, feats in enumerate(BATCHES):
                        for f in feats:
                            nc.gpsimd.indirect_dma_start(
                                out=emb[:, slot, SLOT[f], :], out_offset=None, in_=tables[f],
                                in_offset=bass.IndirectOffsetOnAxis(ap=ids_now[:, slot, f:f + 1], axis=0),
                            ).then_inc(gathered[slot][b], 16)

        @block.tensor
        def _(pe):
            def spread_ids(ph, m, step):
                u = step[1]
                half, n = u // NO % 2, u % NO
                if n == 0:
                    pe.wait_ge(ids16_done, 2 * m + u // NO + 1)
                wait(pe, ids_out, U * m + u)
                for t in range(2):
                    last = nc.tensor.matmul(ids_ps[:, t * P:(t + 1) * P],
                                            ids16[:, 2 * half + t, n:n + 1].to_broadcast([P, P]), ident16[:, :],
                                            start=True, stop=True)
                last.then_inc(ids_full, 1)

            def onehot_unit(ph, m, step):
                u = step[1]
                n = u % NO
                bank = turned[ph.bank(step)]
                if ph is PRO and u < U + NO:
                    pe.wait_ge(hi_done, n + 1)
                    pe.wait_ge(lo_done, n + 1)
                wait(pe, turned_out, ph.free(m, step))
                for k in range(KT):
                    pe.wait_ge(onehot_full, KT * (U * m + u) + k + 1)
                    nc.tensor.matmul(bank[:, 0:HALF], tab_hi[0:RP, n, k, :], onehot[0:RP, k, :],
                                     start=(k == 0), stop=False)
                    nc.tensor.matmul(bank[:, 0:HALF], tab_lo[0:RP, n, k, :], onehot[0:RP, k, :],
                                     start=False, stop=(k == KT - 1)).then_inc(onehot_used, 1)

            def turn_rows(ph, m, step):
                _, t, b = step
                feats = BATCHES[b]
                pe.wait_ge(gathered[t % NS][b], 16 * len(feats) * (T // NS * m + t // NS + 1))
                wait(pe, turned_out, ph.free(m, step))
                for q, f in enumerate(feats):
                    last = nc.tensor.transpose(turned[ph.bank(step)][:, q * P:(q + 1) * P],
                                               emb[:, t % NS, SLOT[f], :], ident[:, :])
                last.then_inc(rows_full, 1)

            def dots_bank(ph, m, step):
                _, t, q = step
                if q == 0:
                    pe.wait_ge(turned_out, ph.tile_out(m, t))
                for n in range(2):
                    wait(pe, dot_out[n], T * NQ * m + NQ * t + q - 1)
                for g in range(GB):
                    at = (q * GB + g) * S
                    four = emb_t[:, t, at:at + S, :]
                    last = nc.tensor.matmul(
                        dot_ps[q % 2][:, g * S * NJ:(g + 1) * S * NJ].rearrange("p (s j) -> p s j", j=NJ),
                        four.rearrange("d s f -> d (s f)"), four[:, :, 1:NF], start=True, stop=True)
                last.then_inc(dot_full, 1)

            def turn_dots(ph, m, step):
                n = step[1]
                bank, banks = turn_bank(ph, n)
                if n == 0:
                    for half in range(2):
                        pe.wait_ge(dot_out[half], T * NQ * (m + 1))
                if n >= banks:
                    pe.wait_ge(turn_out[n % 2], NTURN[n % 2] * m + (n - banks) // 2 + 1)
                for q, j in enumerate(ZB[n]):
                    last = nc.tensor.transpose(bank[:, q * P:(q + 1) * P], dots_v[:, j, :], ident[:, :])
                last.then_inc(turn_full, 1)

            def turn_pairs(m, step, side, half):
                _, h, n = step
                c, w = ZC[n]
                for k in range(2):
                    before = NTURN[k] if side is main and k == n % 2 else TURNS_BEFORE[n][k]
                    pe.wait_ge(turn_out[k], NTURN[k] * m + before)
                if n == len(ZC) - 1:
                    pe.wait_ge(dense_in, 16 * T * (m + 1))
                if n == 2:
                    pe.wait_ge(side.z_lo_out, len(ZC) * half + 1)
                for s in range(2):
                    last = nc.tensor.transpose(side.z_ps[n % 2][0:w, s * P:(s + 1) * P],
                                               z[:, 2 * h + s, c:c + w], ident[:, :])
                last.then_inc(side.pairs_full, 1)

            def product(bank, w_hi, w_lo, x_hi, x_lo, first, final):
                nc.tensor.matmul(bank, w_hi, x_hi, start=first, stop=False)
                nc.tensor.matmul(bank, w_hi, x_lo, start=False, stop=False)
                return nc.tensor.matmul(bank, w_lo, x_hi, start=False, stop=final)

            def mlp(m, step, side, half):
                kind = step[0]
                if kind == "pairs":
                    turn_pairs(m, step, side, half)
                    return
                bank = side.h_ps[hidden_use(step) % 2]
                if kind == "hidden1":
                    n = step[2]
                    if n == 0:
                        pe.wait_ge(side.z_lo_out, len(ZC) * (half + 1))
                        wait(pe, side.h_out, side.h_start + NH * half)
                    if n >= 2:
                        pe.wait_ge(side.h1_lo_out, H1C * half + n - 1)
                    cols = slice(n * P, (n + 1) * P)
                    for c, (_, w) in enumerate(ZC):
                        last = product(bank[:, 0:HALF], w1_hi[0:w, c, cols], w1_lo[0:w, c, cols],
                                       side.z_hi[0:w, c, :], side.z_lo[0:w, c, :], c == 0, c == len(ZC) - 1)
                elif kind == "hidden2":
                    n = step[2]
                    pe.wait_ge(side.h1_lo_out, H1C * (half + 1))
                    cols = slice(n * P, (n + 1) * P)
                    for c in range(H1C):
                        last = product(bank[:, 0:HALF], w2_hi[:, c, cols], w2_lo[:, c, cols],
                                       side.h1_hi[:, c, :], side.h1_lo[:, c, :], c == 0, c == H1C - 1)
                else:
                    pe.wait_ge(side.h_out, side.h_start + NH * half + H2C)
                    for c in range(H2C):
                        last = nc.tensor.matmul(bank[0:1, 0:HALF], w3[:, c:c + 1], side.h2[:, c, :],
                                                start=(c == 0), stop=(c == H2C - 1))
                last.then_inc(side.h_full, 1)

            def run(ph, m):
                for step in ph.steps:
                    if step[0] == "ids":
                        spread_ids(ph, m, step)
                    elif step[0] == "onehot":
                        onehot_unit(ph, m, step)
                    elif step[0] == "rows":
                        turn_rows(ph, m, step)
                    elif step[0] == "dots":
                        dots_bank(ph, m, step)
                    elif step[0] == "turn":
                        turn_dots(ph, m, step)
                    else:
                        mlp(m - 1, step, main, 2 * (m - 1) + step[1])

            pe.wait_ge(ident16_done, 1)
            pe.wait_ge(ident_done, 1)
            run(PRO, -1)
            pe.wait_ge(pads_done, 1)
            run(FIRST, 0)
            pe.wait_ge(weights_in, 16 * 2)
            pe.wait_ge(w_hi_done, 3)
            pe.wait_ge(w_lo_done, 3)
            pe.wait_ge(ones_done, 1)
            with pe.Fori(1, NM - 1) as m:
                run(BODY, m)
            run(LAST, NM - 1)
            for step in TAIL:
                mlp(NM - 1, step, *side_of_tail(step))

        @block.scalar
        def _(act):
            with nc.allow_non_contiguous_dma(reason="512 single words, once"):
                act.dma_start(w3[:, :], w_top3.rearrange("(c p) o -> p (c o)", p=P)).then_inc(weights_in, 16)
                act.dma_start(b2[:, :], b_top2.rearrange("(c p) -> p c", p=P)).then_inc(weights_in, 16)

            def table_high(n):
                act.wait_ge(raw_in[n % NRAW], 32 * (n // NRAW + 1))
                nc.scalar.copy(tab_hi[0:RP, n, :, :], raw[n % NRAW].rearrange("p (k d) -> p k d", k=KT)
                               ).then_inc(hi_done, 1)

            def copy_ids(ph, m, step):
                u = step[1]
                if ph is PRO and u < U + NO:
                    table_high(u - U)
                act.wait_ge(ids_full, U * m + u + 1)
                if ph is not PRO or u >= U + 2:
                    act.wait_ge(onehot_full, KT * (U * m + u - 1))
                nc.scalar.copy(idsb[:, u % 2, :], ids_ps[:, :]).then_inc(ids_out, 1)

            def onehot_out(ph, m, step):
                u = step[1]
                half, n = u // NO % 2, u % NO
                act.wait_ge(onehot_used, KT * (U * m + u + 1))
                nc.scalar.copy(emb_t[:, 2 * half:2 * half + 2, :, ONEHOT[n]],
                               turned[ph.bank(step)][:, 0:HALF].rearrange("d (t p) -> d t p", t=2)
                               ).then_inc(turned_out, 1)

            def rows_out(ph, m, step):
                _, t, b = step
                feats = BATCHES[b]
                act.wait_ge(rows_full, ph.filled(m, step))
                dst = batch_view(emb_t[:, t % T, :, :].rearrange("d p f -> d f p"), feats)
                src = turned[ph.bank(step)][:, 0:len(feats) * P]
                if len(dst.shape) == 4:
                    src = src.rearrange("d (a b p) -> d a b p", a=2, b=2)
                else:
                    src = src.rearrange("d (q p) -> d q p", p=P)
                nc.scalar.copy(dst, src).then_inc(turned_out, 1)

            def dots_out(m, step):
                _, t, q = step
                act.wait_ge(dot_full, T * NQ * m + NQ * t + q + 1)
                for s in (2, 3):
                    last = nc.scalar.copy(*own_dots(t, q, s))
                last.then_inc(dot_out[1], 1)

            def mlp_out(m, step, side, half):
                kind, h = step[0:2]
                if kind == "pairs":
                    n = step[2]
                    w = ZC[n][1]
                    act.wait_ge(side.pairs_full, len(ZC) * half + n + 1)
                    nc.scalar.copy(side.z_hi[0:w, n, :], side.z_ps[n % 2][0:w, 0:HALF]).then_inc(side.z_hi_out, 1)
                    return
                bank = side.h_ps[hidden_use(step) % 2]
                act.wait_ge(side.h_full, NU * half + hidden_use(step) + 1)
                if kind == "hidden1":
                    nc.scalar.activation(side.h1_hi[:, step[2], :], bank[:, 0:HALF], ACT.Relu
                                         ).then_inc(side.h1_hi_out, 1)
                elif kind == "hidden2":
                    n = step[2]
                    if n == 0:
                        wait(act, side.y_sent, 16 * (half + side.h_start))
                    nc.scalar.activation(side.h2[:, n, :], bank[:, 0:HALF], ACT.Relu, bias=b2[:, n:n + 1]
                                         ).then_inc(side.h_out, 1)
                else:
                    nc.scalar.copy(side.y.rearrange("o (g s t) -> o s t g", s=2, t=T),
                                   bank[0:1, 0:HALF].rearrange("o (s t g) -> o s t g", s=2, t=T)).then_inc(side.h_out, 1)

            def weights_high(n):
                rows, src, hi, _ = W_PARTS[n]
                act.wait_ge(w_raw_in, W_COUNT[n])
                dst = hi[0:rows]
                src = src[0:rows, :]
                if len(dst.shape) == 3:
                    src = src.rearrange("p (c h) -> p c h", c=dst.shape[1])
                nc.scalar.copy(dst, src).then_inc(w_hi_done, 1)

            def run(ph, m):
                for step in ph.steps:
                    if step[0] == "ids":
                        copy_ids(ph, m, step)
                    elif step[0] == "onehot":
                        onehot_out(ph, m, step)
                    elif step[0] == "rows":
                        rows_out(ph, m, step)
                    elif step[0] == "dots":
                        dots_out(m, step)
                        if ph is FIRST and step[2] == NQ - 1 and step[1] < len(W_PARTS):
                            weights_high(step[1])
                    elif step[0] == "turn":
                        if ph is FIRST and step[1] == 1:
                            act.wait_ge(w_lo_done, len(W_PARTS))
                        if step[1] % 2 == 1:
                            turned_dots_out(act, nc.scalar.copy, ph, m, step)
                    else:
                        mlp_out(m - 1, step, main, 2 * (m - 1) + step[1])

            run(PRO, -1)
            act.wait_ge(weights_in, 16 * 2)
            run(FIRST, 0)
            with act.Fori(1, NM - 1) as m:
                run(BODY, m)
            run(LAST, NM - 1)
            for step in TAIL:
                mlp_out(NM - 1, step, *side_of_tail(step))

        @block.vector
        def _(dve):
            def ids_for_tile(m, t):
                if isinstance(m, int) and T * m + t >= NM * T:
                    return
                nc.vector.tensor_copy(ids_now[:, t % NS, :],
                                      ids_sb[:, bass.ds(m * T + t, 1), :].rearrange("p m f -> p (m f)")
                                      ).then_inc(tile_open[t % NS], 1)

            def ids_to_fp16(m, half):
                for n0, n1 in IDS_RUNS:
                    f0, f1 = ONEHOT[n0], ONEHOT[n1 - 1]
                    last = nc.vector.tensor_copy(ids16[:, 2 * half:2 * half + 2, n0:n1],
                                                 ids_sb[:, bass.ds((m + 1) * T + 2 * half, 2),
                                                        f0:f1 + 1:ONEHOT[n0 + 1] - f0])
                last.then_inc(ids16_done, 1)

            def columns(ph, m, u):
                if ph is PRO and u < U + NO:
                    table_low(u - U)
                dve.wait_ge(ids_out, U * m + u + 1)
                for k in range(KT):
                    wait(dve, onehot_used, KT * (U * m + u - 1) + k + 1)
                    nc.vector.tensor_scalar(onehot[0:RP, k, :], idsb[0:RP, u % 2, :], rowid[0:RP, k:k + 1],
                                            None, ALU.is_equal).then_inc(onehot_full, 1)

            def dots_out(m, step):
                _, t, q = step
                dve.wait_ge(dot_full, T * NQ * m + NQ * t + q + 1)
                for s in (0, 1):
                    last = nc.vector.tensor_copy(*own_dots(t, q, s))
                last.then_inc(dot_out[0], 1)
                if q == 0:
                    ids_for_tile(m, t + NS)

            def mlp_low(step, side, half):
                if step[0] == "pairs":
                    n = step[2]
                    w = ZC[n][1]
                    dve.wait_ge(side.z_hi_out, len(ZC) * half + n + 1)
                    nc.vector.tensor_tensor(side.z_lo[0:w, n, :], side.z_ps[n % 2][0:w, 0:HALF],
                                            side.z_hi[0:w, n, :].bitcast(fp32), ALU.subtract).then_inc(side.z_lo_out, 1)
                elif step[0] == "hidden1":
                    n = step[2]
                    dve.wait_ge(side.h1_hi_out, H1C * half + n + 1)
                    nc.vector.scalar_tensor_tensor(out=side.h1_lo[:, n, :], in0=side.h_ps[hidden_use(step) % 2][:, 0:HALF],
                                                   scalar=0.0, in1=side.h1_hi[:, n, :].bitcast(fp32),
                                                   op0=ALU.max, op1=ALU.subtract).then_inc(side.h1_lo_out, 1)

            def weights_low(n):
                rows, src, hi, lo = W_PARTS[n]
                dve.wait_ge(w_hi_done, n + 1)
                flat = (lambda ap: ap[0:rows].rearrange("p c h -> p (c h)")) if n != 1 else (lambda ap: ap[0:rows])
                nc.vector.tensor_tensor(flat(lo), src[0:rows, :], flat(hi).bitcast(fp32), ALU.subtract
                                        ).then_inc(w_lo_done, 1)
                if n == len(W_PARTS) - 1:
                    dve.wait_ge(w_lo_done, n + 1)
                    nc.vector.memset(z[:, :, KZ - 1:KZ], 1.0).then_inc(ones_done, 1)

            def table_low(n):
                dve.wait_ge(hi_done, n + 1)
                nc.vector.tensor_tensor(tab_lo[0:RP, n, :, :].rearrange("p k d -> p (k d)"), raw[n % NRAW],
                                        tab_hi[0:RP, n, :, :].rearrange("p k d -> p (k d)").bitcast(fp32),
                                        ALU.subtract).then_inc(lo_done, 1)

            def run(ph, m):
                for step in ph.for_dve():
                    if step[0] == "columns":
                        columns(ph, m, step[1])
                    elif step[0] == "ids16":
                        ids_to_fp16(m, step[1])
                    elif step[0] == "dots":
                        dots_out(m, step)
                        if ph is FIRST and step[2] == NQ - 1 and step[1] < len(W_PARTS):
                            weights_low(step[1])
                    elif step[0] == "turn":
                        if step[1] % 2 == 0:
                            turned_dots_out(dve, nc.vector.tensor_copy, ph, m, step)
                    else:
                        mlp_low(step, main, 2 * (m - 1) + step[1])

            nc.vector.memset(ident[:, :], 0.0).then_inc(ident_zero, 1)
            nc.vector.memset(start[:, 0:1], 0.0).then_inc(main.y_sent, 16)
            nc.vector.memset(start[:, 1:2], 0.0).then_inc(main.h_out, 1)
            dve.wait_ge(ids_in, 16)
            for t in range(NS):
                ids_for_tile(0, t)
            ids_to_fp16(-1, 0)
            ids_to_fp16(-1, 1)
            dve.wait_ge(ident_done, 1)
            nc.vector.tensor_copy(ident16[:, :], ident[:, :]).then_inc(ident16_done, 1)
            nc.vector.memset(emb_t[:, :, :, NF:ROW], 0.0).then_inc(pads_done, 1)
            dve.wait_ge(rowid_done, 1)
            run(PRO, -1)
            dve.wait_ge(lo_done, NO)
            dve.wait_ge(ids_rest_in, 16)
            run(FIRST, 0)
            with dve.Fori(1, NM - 1) as m:
                run(BODY, m)
            run(LAST, NM - 1)
            for step in TAIL:
                mlp_low(step, *side_of_tail(step))


_INS = ["dense_ctx", "ids"] + [f"tbl_{i}" for i in range(27)] + ["W_top1", "b_top1", "W_top2", "b_top2", "W_top3"]


def kernel(**inputs):
    import numpy as _np
    import concourse.bacc as _bacc
    from concourse import mybir as _mybir
    from concourse.bass_utils import run_bass_kernel_spmd as _run

    nc = _bacc.Bacc("TRN2", target_bir_lowering=False, num_devices=1)
    arrays, args = {}, {}
    for name in _INS:
        a = _np.ascontiguousarray(inputs[name])
        arrays[f"in_{name}_dram"] = a
        args[name] = nc.dram_tensor(f"in_{name}_dram", a.shape, _mybir.dt.from_np(a.dtype), kind="ExternalInput").ap()
    batch = inputs["ids"].shape[0]
    out = nc.dram_tensor("out_0_dram", (batch, 1), _mybir.dt.float32, kind="ExternalOutput").ap()
    dlrm_tower(nc, args["dense_ctx"], args["ids"], [args[f"tbl_{i}"] for i in range(27)],
               args["W_top1"], args["b_top1"], args["W_top2"], args["b_top2"], args["W_top3"], out)
    r = _run(nc, [arrays], core_ids=[0])
    return r.results[0]["out_0_dram"]
```
